# Optimizing a Trainium2 kernel written in Bass

```python
import numpy as np
import jax
import jax.numpy as jnp

def _softmax(x, axis=-1):
    return jax.nn.softmax(x, axis=axis)
def _gelu(x):
    return jax.nn.gelu(x, approximate=True)
def _silu(x):
    return jax.nn.silu(x)
def _sigmoid(x):
    return jax.nn.sigmoid(x)
def _layernorm(x, axis=-1, eps=1e-5):
    m = jnp.mean(x, axis=axis, keepdims=True)
    v = jnp.var(x, axis=axis, keepdims=True)
    return (x - m) / jnp.sqrt(v + eps)
def _scatter_add(tgt, idx, src, axis=0):
    return tgt.at[idx].add(src)
def _segment_sum(src, seg, n):
    return jax.ops.segment_sum(src, seg, n)

kernel_name = 'mk_adj_preln_d1_adj_256_b18c82'

def setup_inputs(seed: int = 0):
    np.random.seed(seed)
    _w = jnp.asarray
    def _rec_inputs():
        import jax
        import jax.numpy as jnp
        _gk = jax.random.key(seed)
        x = -0.000929 + 1 * jax.random.normal(jax.random.fold_in(_gk, 1), (8192, 256), jnp.float32)
        _w = (1.0 + jnp.arange(8192, dtype=jnp.float32)) ** -0.5
        _w = _w / _w.mean()
        _pij = jnp.clip(0.00195312 * _w[:, None] * _w[None, :], 0.0, 1.0)
        _a = jax.random.uniform(jax.random.fold_in(_gk, 2), (8192, 8192)) < _pij
        _a = jnp.logical_or(_a, jnp.eye(8192, dtype=bool))
        _af = _a.astype(jnp.float32)
        _af = _af * jax.random.uniform(jax.random.fold_in(_gk, 3), (8192, 8192), jnp.float32, 0.05, 1)
        adj = _af
        return x, adj
    x, adj = _rec_inputs()
    def _L0_gnn_setup():
        import jax, jax.numpy as jnp
        import numpy as np
        N = 4096
        IN = 256
        H = 8
        D = 32
        ALPHA = 0.2
        key = jax.random.key(seed)
        ks = jax.random.split(key, 9)
        xav = lambda k, sh: jax.random.normal(k, sh, jnp.float32) * np.float32(np.sqrt(2.0 / (sh[0] + sh[-1])))
        return {'x': jax.random.normal(ks[0], (N, IN), jnp.float32), 'adj_matrix': jax.random.uniform(ks[1], (N, N), jnp.float32), 'W': xav(ks[2], (H * D, IN)), 'We': xav(ks[3], (H, 1)), 'be': jnp.zeros((H,), jnp.float32), 'a_src': xav(ks[4], (H, D)), 'a_dst': xav(ks[5], (H, D)), 'Wr': xav(ks[6], (H * D, IN)), 'br': jnp.zeros((H * D,), jnp.float32)}
    _L0_gnn_all = _L0_gnn_setup()
    _L0_gnn_in = {k: v for k, v in _L0_gnn_all.items() if k in ('W', 'We', 'be', 'a_src', 'a_dst', 'Wr', 'br', )}
    del _L0_gnn_all

    return {
        "x": x,
        "adj": adj,
        "L0_gnn_W": _L0_gnn_in["W"],
        "L0_gnn_We": _L0_gnn_in["We"],
        "L0_gnn_be": _L0_gnn_in["be"],
        "L0_gnn_a_src": _L0_gnn_in["a_src"],
        "L0_gnn_a_dst": _L0_gnn_in["a_dst"],
        "L0_gnn_Wr": _L0_gnn_in["Wr"],
        "L0_gnn_br": _L0_gnn_in["br"],
    }

def reference(x, adj, L0_gnn_W, L0_gnn_We, L0_gnn_be, L0_gnn_a_src, L0_gnn_a_dst, L0_gnn_Wr, L0_gnn_br):
    import jax
    import jax.numpy as jnp
    def _L0_gnn_ref(x, adj_matrix, W, We, be, a_src, a_dst, Wr, br):
        import jax, jax.numpy as jnp
        import numpy as np
        N = 4096
        IN = 256
        H = 8
        D = 32
        ALPHA = 0.2
        n = x.shape[0]
        h = (x @ W.T).reshape(n, H, D)
        s_src = jnp.einsum('nhd,hd->nh', h, a_src)
        s_dst = jnp.einsum('nhd,hd->nh', h, a_dst)
        attn = s_src[:, None, :] + s_dst[None, :, :]
        attn = attn + adj_matrix[:, :, None] * We[:, 0] + be
        mask = (adj_matrix > 0)[:, :, None]
        attn = jnp.where(mask, attn, -jnp.inf)
        attn = jax.nn.leaky_relu(attn, ALPHA)
        attn = jax.nn.softmax(attn, axis=1)
        h_out = jnp.einsum('ijh,jhd->ihd', attn, h).reshape(n, H * D)
        return h_out + x @ Wr.T + br

    h = jnp.maximum(_layernorm(x, axis=-1), 0.0)
    x = x + _L0_gnn_ref(h, adj, L0_gnn_W, L0_gnn_We, L0_gnn_be, L0_gnn_a_src, L0_gnn_a_dst, L0_gnn_Wr, L0_gnn_br)
    return x


_drawn_inputs = setup_inputs


def setup_inputs(seed=0):
    import zlib

    import numpy as np

    out = dict(_drawn_inputs(seed))
    spreads = {'L0_gnn_be': (0.0, 2.0), 'L0_gnn_br': (0.0, 0.1)}
    factors = {'L0_gnn_We': 2.95, 'L0_gnn_a_src': 2.996}
    for name, (base, spread) in spreads.items():
        noise = np.random.default_rng([zlib.crc32(name.encode()), seed]).standard_normal(out[name].shape)
        drawn = base * np.exp(spread * noise) if base else spread * noise
        out[name] = jnp.asarray(drawn.astype(out[name].dtype))
    for name, factor in factors.items():
        out[name] = (out[name] * factor).astype(out[name].dtype)
    return out
```

```python
from contextlib import ExitStack

import numpy as np
import concourse.bass as bass
from concourse import mybir

ALU = mybir.AluOpType
ACT = mybir.ActivationFunctionType
F32 = mybir.dt.float32
U32 = mybir.dt.uint32
I32 = mybir.dt.int32
AX_X = mybir.AxisListType.X

P = 128
N = 8192
IN = 256
H = 8
D = 32
HD = H * D
TILES = N // P
ROW = HD + H
ALPHA = 0.2
EPS = 1e-5
NEG = -1e30
PAD = 64
JBITS = 17
LOW = (1 << JBITS) - 1
GSLOTS = 96

FIRST = 2
PHASES = [(2, 4, 64, 48), (4, 8, 56, 48), (8, 16, 40, 16), (16, 32, 32, 16), (32, 64, 24, 16)]
KMAX = max(p[2] for p in PHASES)
VMAX = 8 * max(p[3] for p in PHASES)


def segments(n):
    bounds = [0]
    for s in range(1, n + 1):
        bounds.append(max(bounds[-1] + 8, int(round(N * (s / n) ** 2))))
    return bounds


def gat_kernel(nc, x, adj, W, We, be, a_src, a_dst, Wr, br, out):
    table = nc.dram_tensor("table", (N + PAD, ROW), F32, kind="Internal").ap()
    resid = nc.dram_tensor("resid", (N, HD), F32, kind="Internal").ap()
    dst_rows = nc.dram_tensor("dst_rows", (H, N), F32, kind="Internal").ap()

    with ExitStack() as ctx:
        def sb(name, shape, dt=F32):
            return ctx.enter_context(nc.sbuf_tensor(name, shape, dt))

        def sem(name):
            return ctx.enter_context(nc.semaphore(name))

        banks = ctx.enter_context(nc.psum_tensor("banks", [P, 8, 512], F32))
        ps_hnT = banks[:, 0:2, 0:IN]
        ps_hd = banks[:, 2:4, 0:ROW + H]
        ps_dst = banks[:, 2:4, 384:512]
        ps_res = banks[:, 4:6, 0:HD]
        ps_w, ps_w2 = banks[:, 6, :], banks[:, 7, :]
        ps_sum = banks[:, 0:2, 0:HD]
        ps_pt = banks[:, 2:4, :]
        ps_out = banks[:, 4:6, 0:D]
        ps_flag, ps_flag_row = banks[:, 6, :], banks[:, 7, :]

        ident = sb("ident", [P, P])
        ones = sb("ones", [P, P])
        w_all = sb("w_all", [P, 2, 528])
        eps = sb("eps", [P, 1])
        brow = sb("brow", [1, HD])
        be_all = sb("be_all", [P, H])
        we_all = sb("we_all", [P, H])
        seg_base = {n: sb(f"seg_base{n}", [P, n * 8]) for n in sorted({p[3] for p in PHASES})}
        s_all = sb("s_all", [P, TILES, H])
        flags = sb("flags", [P, TILES])
        flagT = sb("flagT", [TILES, 1])
        flag_row = sb("flag_row", [1, TILES], I32)

        adj_sb = sb("adj_sb", [P, 2, N])
        gath = sb("gath", [P, GSLOTS, ROW])
        val8 = sb("val8", [P, VMAX])
        idx8 = sb("idx8", [P, VMAX], U32)
        jpad = sb("jpad", [P, VMAX], U32)
        key_lo = sb("key_lo", [P, VMAX], U32)
        key_hi = sb("key_hi", [P, VMAX], U32)
        slot_lo = sb("slot_lo", [P, KMAX], U32)
        slot_hi = sb("slot_hi", [P, KMAX], U32)
        jcol = sb("jcol", [P, KMAX], U32)
        far = sb("far", [P, KMAX])
        offs = sb("offs", [P, 2, KMAX], U32)
        aval = sb("aval", [P, KMAX], U32)
        ahi = sb("ahi", [P, KMAX], U32)
        off_mask = sb("off_mask", [P, KMAX])
        pre = sb("pre", [P, 2, KMAX * H])
        z = sb("z", [P, KMAX * H])
        prob = sb("prob", [P, KMAX * H])
        flag8 = sb("flag8", [P, 1])
        rmax = sb("rmax", [P, H])
        rsum = sb("rsum", [P, H])
        rinv = sb("rinv", [P, H])
        res_sb = sb("res_sb", [P, 2, HD])
        out_sb = sb("out_sb", [P, 2, HD])

        gflat = gath[:, :, :].rearrange("p k r -> p (k r)")
        at = [0]

        def part(width):
            at[0] += width
            return gflat[:, at[0] - width:at[0]]

        w_sb = part(2 * IN).rearrange("p (q n) -> p q n", q=2)
        wr_sb = part(2 * IN).rearrange("p (q n) -> p q n", q=2)
        a_blk = part(32).rearrange("p (q n) -> p q n", q=2)
        x_sb = part(2 * IN).rearrange("p (b n) -> p b n", b=2)
        hn = part(2 * IN).rearrange("p (b n) -> p b n", b=2)
        hnT = part(2 * IN).rearrange("p (b n) -> p b n", b=2)
        hd_sb = part(2 * (ROW + H)).rearrange("p (b n) -> p b n", b=2)
        rt_sb = part(2 * HD).rearrange("p (b n) -> p b n", b=2)
        dst_sb = part(2 * P).rearrange("p (b n) -> p b n", b=2)
        stat = part(12)
        mv = part(4)
        rstd = part(2)
        sdev = part(2)
        bias_m = gflat[:, 0:N]
        dst_bc = gflat[:, N:2 * N]
        u_sb = [adj_sb[:, 1, :], gflat[:, 2 * N:3 * N]]
        a_t = adj_sb[:, 0, :]
        pt_sb = pre[:, :, 0:512]
        h_sb = sb("h_sb", [P, TILES * D])
        umax = sb("umax", [P, 2])
        ushift = sb("ushift", [P, 2])
        uleak = sb("uleak", [P, 2])
        nmax = sb("nmax", [P, 2])
        uden = sb("uden", [P, 2])
        urec = sb("urec", [P, 2])
        dres = sb("dres", [P, HD])
        dout = sb("dout", [P, HD])

        S = {n: sem(n) for n in (
            "ones_set", "held", "ident_set", "blk_zero", "blk_in", "w_in", "small_in", "wt_done", "wt_copied",
            "x_in0", "x_in1", "x_free", "bn_done", "mv_done", "sd_done", "eps_set", "rstd_done", "hn_done", "hnT_ps", "hnT_done",
            "proj_done", "hd_copied", "dst_copied", "s_done", "res_done",
            "hd_out0", "hd_out1", "res_out0", "res_out1", "dst_out0", "dst_out1", "gath_zero", "pad_out", "base_set",
            "adj_in0", "adj_in1", "maxed", "scanned", "jadd", "jshift", "keyed", "masked_keys", "sorted_",
            "dec1", "dec2", "dec3", "decoded", "az1", "az2", "pre_done", "offs_ready", "flag_a", "flag_b",
            "gath_in0", "gath_in1", "z1", "z2", "z3", "z_ready", "exped", "summed_p", "recip", "normed",
            "weighted", "tile_sum", "out_copied", "out_st0", "out_st1", "res_in0", "res_in1",
            "fl_t", "fl_max", "fl_row", "fl_ready", "flag_init",
            "d_adj", "d_free", "d_mask", "d_dst", "d_h", "d_u1", "d_u2", "d_m1", "d_m2", "d_m", "d_leak", "d_src", "d_exp",
            "d_tr", "d_ev", "d_used", "d_pv", "d_rec", "d_fin", "d_res", "d_out")}

        def hold(eng, semaphore, value):
            eng.wait_ge(semaphore, value)
            eng.sem_inc(S["held"], 1)

        load_adj = lambda t: adj[bass.ts(t, P), :]
        block = ctx.enter_context(nc.Block())

        @block.sync
        def _(sp):
            sp.dma_start(w_sb, W.rearrange("(q p) n -> p q n", p=P)).then_inc(S["w_in"], 16)
            sp.dma_start(wr_sb, Wr.rearrange("(q p) n -> p q n", p=P)).then_inc(S["w_in"], 16)
            sp.dma_start(brow[:, :], br.rearrange("(a n) -> a n", a=1)).then_inc(S["small_in"], 16)
            sp.dma_start(be_all[:, :], be.partition_broadcast(P)).then_inc(S["small_in"], 16)
            sp.dma_start(we_all[:, :], We.rearrange("h a -> (h a)").partition_broadcast(P)).then_inc(S["small_in"], 16)
            sp.wait_ge(S["blk_zero"], 1)
            for q in range(2):
                for r in range(4):
                    h = 4 * q + r
                    for o, a in ((0, a_dst), (H, a_src)):
                        sp.dma_start(a_blk[D * r:D * r + D, q, o + h:o + h + 1],
                                     a[h, :].rearrange("(d a) -> d a", a=1)).then_inc(S["blk_in"], 16)
            with sp.Fori(0, TILES // 2) as i:
                for b in range(2):
                    t = 2 * i + b
                    sp.wait_ge(S["x_free"], t + 1)
                    sp.dma_start(x_sb[:, b, :], x[bass.ts(t, P), :]).then_inc(S[f"x_in{b}"], 16)
            c = 0
            for t0, t1, K, NS in PHASES:
                def load(t, c, b):
                    sp.dma_start(adj_sb[:, b, :], load_adj(t)).then_inc(S[f"adj_in{b}"], 16)
                if t0 == FIRST:
                    for t in range(t0, t1):
                        if c >= 2:
                            sp.wait_ge(S["scanned"], c - 1)
                        load(t, c, t % 2)
                        c += 1
                else:
                    with sp.Fori(0, (t1 - t0) // 2) as i:
                        for b in range(2):
                            sp.wait_ge(S["scanned"], 2 * i + (c + b - 1))
                            load(2 * i + (t0 + b), c, b)
                    c += t1 - t0
            sp.sem_inc(S["d_free"], 1)
            sp.sem_inc(S["d_u1"], 1)
            done = sp.alloc_register("dense_sp")
            sp.reg_mov(done, 0)
            sp.wait_ge(S["fl_ready"], 1)
            with sp.Fori(0, TILES) as t:
                flag = sp.value_load(flag_row[0:1, bass.ds(t, 1)], min_val=0, max_val=1)
                with sp.If(flag > 0):
                    n = sp.snap(done)
                    sp.wait_ge(S["d_free"], n + 1)
                    sp.dma_start(a_t, load_adj(t)).then_inc(S["d_adj"], 16)
                    sp.dma_start(dres[:, :], resid[bass.ts(t, P), :]).then_inc(S["d_res"], 16)
                    with sp.Fori(0, H // 2) as hp:
                        for b in range(2):
                            g = n * H + hp * 2 + b
                            h = hp * 2 + b
                            sp.wait_ge(S["d_u1"], g + 1)
                            sp.dma_start(dst_bc, dst_rows[bass.ds(h, 1), :].partition_broadcast(P)[:, 0, :]).then_inc(S["d_dst"], 16)
                            sp.wait_ge(S["d_pv"], g + 2)
                            sp.dma_start(h_sb[:, :].rearrange("p (c d) -> p c d", d=D),
                                         table[PAD:, :].rearrange("(c p) r -> p c r", p=P)[:, :, bass.ts(h, D)]
                                         ).then_inc(S["d_h"], 16)
                    sp.reg_add(done, done, 1)

        @block.gpsimd
        def _(pool):
            pool.memset(ones[:, :], 1.0).then_inc(S["ones_set"], 1)
            pool.memset(eps[:, :], EPS).then_inc(S["eps_set"], 1)
            pool.memset(a_blk, 0.0).then_inc(S["blk_zero"], 1)
            pool.memset(flags[:, :], 1.0).then_inc(S["flag_init"], 1)
            for n, base in seg_base.items():
                bounds = segments(n)
                for s in range(n):
                    last = pool.memset(base[:, 8 * s:8 * s + 8], float(bounds[s] + PAD))
            last.then_inc(S["base_set"], 1)
            pool.wait_ge(S["ones_set"], 1)
            pool.affine_select(out=ident[:, :], in_=ones[:, :], compare_op=ALU.is_equal, fill=0.0,
                               base=0, pattern=[[-1, P]], channel_multiplier=1).then_inc(S["ident_set"], 1)
            with pool.Fori(0, TILES // 2) as i:
                for b in range(2):
                    t = 2 * i + b
                    pool.wait_ge(S["hd_copied"], t + 1)
                    pool.dma_start(table[PAD:, :].rearrange("(t p) r -> t p r", p=P)[bass.ds(t, 1), :, :]
                                   .rearrange("a p r -> (a p) r"), hd_sb[:, b, 0:ROW]).then_inc(S[f"hd_out{b}"], 16)
                    pool.wait_ge(S["dst_copied"], t + 1)
                    pool.dma_start(dst_rows[:, bass.ts(t, P)], dst_sb[0:H, b, :]).then_inc(S[f"dst_out{b}"], 16)
                    pool.wait_ge(S["res_done"], t + 1)
                    pool.dma_start(resid[bass.ts(t, P), :], rt_sb[:, b, :]).then_inc(S[f"res_out{b}"], 16)
            for b in range(2):
                for q in ("hd_out", "dst_out", "res_out"):
                    pool.wait_ge(S[f"{q}{b}"], 16 * (TILES // 2))
            pool.memset(gflat, 0.0).then_inc(S["gath_zero"], 1)
            pool.wait_ge(S["gath_zero"], 1)
            pool.dma_start(table[0:PAD, :], gath[0:PAD, 0, :]).then_inc(S["pad_out"], 16)
            pool.wait_ge(S["pad_out"], 16)
            c = 0
            single = False
            for t0, t1, K, NS in PHASES:
                if single and K <= GSLOTS // 2:
                    pool.wait_ge(S["tile_sum"], c)
                single = K > GSLOTS // 2

                def gather(i):
                    for b in range(2):
                        if not isinstance(i, int) or c + b:
                            pool.wait_ge(S["tile_sum"], 2 * i + (c + b - (0 if single else 1)))
                        hold(pool, S["offs_ready"], 2 * i + (c + b + 1))
                        g0 = 0 if single else b * (GSLOTS // 2)
                        for k in range(K):
                            pool.indirect_dma_start(
                                gath[:, g0 + k, :], None, table[:, :],
                                bass.IndirectOffsetOnAxis(ap=offs[:, b, k:k + 1], axis=0),
                                bounds_check=N + PAD - 1, oob_is_err=False).then_inc(S[f"gath_in{b}"], 16)

                if t1 - t0 == 2:
                    gather(0)
                else:
                    with pool.Fori(0, (t1 - t0) // 2) as i:
                        gather(i)
                c += t1 - t0

        def gather_counts():
            base, at = [], 0
            for t0, t1, K, NS in PHASES:
                base.append(at)
                at += (t1 - t0) // 2 * 16 * K
            return base

        @block.vector
        def _(dve):
            v = nc.vector
            for c in range(2):
                dve.wait_ge(S["wt_done"], c + 1)
                v.tensor_copy(w_all[:, c, 0:HD], ps_w[:, 0:HD])
                v.tensor_copy(w_all[:, c, 272:528], ps_w[:, HD:2 * HD])
                v.tensor_copy(w_all[:, c, HD:HD + 16], ps_w2[:, 0:16]).then_inc(S["wt_copied"], 1)
            dve.sem_inc(S["x_free"], 2)
            dve.wait_ge(S["small_in"], 48)

            def project(i):
                for b in range(2):
                    t = 2 * i + b
                    dve.wait_ge(S[f"x_in{b}"], 16 * i + 16)
                    v.bn_stats(stat[:, 6 * b:6 * b + 6], x_sb[:, b, :]).then_inc(S["bn_done"], 1)
                    hold(dve, S["bn_done"], t + 1)
                    v.bn_aggr(mv[:, 2 * b:2 * b + 2], stat[:, 6 * b:6 * b + 6]).then_inc(S["mv_done"], 1)
                    dve.wait_ge(S["sd_done"], t + 1)
                    v.reciprocal(rstd[:, b:b + 1], sdev[:, b:b + 1]).then_inc(S["rstd_done"], 1)
                    dve.wait_ge(S["rstd_done"], t + 1)
                    v.tensor_scalar(hn[:, b, :], x_sb[:, b, :], mv[:, 2 * b:2 * b + 1], rstd[:, b:b + 1],
                                    ALU.subtract, ALU.mult).then_inc(S["hn_done"], 1)
                    dve.wait_ge(S["hd_copied"], t + 1)
                    v.tensor_tensor(s_all[:, bass.ds(t, 1), :].rearrange("p a h -> p (a h)"),
                                    hd_sb[:, b, ROW:ROW + H], be_all[:, :], ALU.add).then_inc(S["s_done"], 1)
                    if not isinstance(i, int):
                        dve.wait_ge(S[f"res_out{b}"], 16 * i)
                    v.tensor_tensor(rt_sb[:, b, :], ps_res[:, b, :], x_sb[:, b, :], ALU.add
                                    ).then_inc(S["res_done"], 1)
                    hold(dve, S["res_done"], t + 1)
                    dve.sem_inc(S["x_free"], 1)

            project(0)
            with dve.Fori(1, TILES // 2) as i:
                project(i)

            dve.wait_ge(S["base_set"], 1)
            dve.wait_ge(S["flag_init"], 1)
            dve.wait_ge(S["s_done"], TILES)
            bases = gather_counts()
            rounds_before = []
            r = 0
            for t0, t1, K, NS in PHASES:
                rounds_before.append(r)
                r += (t1 - t0) * (2 * (K // 8))

            def scan(ph, j, b):
                t0, t1, K, NS = PHASES[ph]
                c = j + (t0 - FIRST)
                VN = 8 * NS
                bounds = segments(NS)
                hold(dve, S[f"adj_in{b}"], (c // 2 if isinstance(c, int) else c >> 1) * 16 + 16)
                a = adj_sb[:, b, :]
                for s in range(NS):
                    last = v.max(val8[:, 8 * s:8 * s + 8], a[:, bounds[s]:bounds[s + 1]])
                last.then_inc(S["maxed"], 1)
                hold(dve, S["maxed"], c + 1)
                for s in range(NS):
                    last = v.max_index(idx8[:, 8 * s:8 * s + 8], val8[:, 8 * s:8 * s + 8],
                                       a[:, bounds[s]:bounds[s + 1]])
                last.then_inc(S["scanned"], 1)
                v.tensor_reduce(flag8[:, :], val8[:, 0:VN].rearrange("p (s e) -> p s e", e=8)[:, :, 7],
                                AX_X, ALU.max).then_inc(S["flag_a"], 1)
                dve.wait_ge(S["scanned"], c + 1)
                v.tensor_tensor(jpad[:, 0:VN], idx8[:, 0:VN], seg_base[NS][:, :], ALU.add).then_inc(S["jadd"], 1)
                dve.wait_ge(S["jadd"], c + 1)
                v.tensor_scalar(idx8[:, 0:VN], jpad[:, 0:VN], JBITS, None, ALU.logical_shift_left
                                ).then_inc(S["jshift"], 1)
                dve.wait_ge(S["jshift"], c + 1)
                vb = val8[:, 0:VN].bitcast(U32)
                v.scalar_tensor_tensor(out=key_lo[:, 0:VN], in0=vb, scalar=LOW, in1=idx8[:, 0:VN],
                                       op0=ALU.bitwise_and, op1=ALU.bitwise_or)
                v.scalar_tensor_tensor(out=key_hi[:, 0:VN], in0=vb, scalar=JBITS, in1=idx8[:, 0:VN],
                                       op0=ALU.logical_shift_right, op1=ALU.bitwise_or).then_inc(S["keyed"], 1)
                dve.wait_ge(S["keyed"], c + 1)
                kl, kh = key_lo[:, 0:VN].bitcast(F32), key_hi[:, 0:VN].bitcast(F32)
                for k in (kl, kh):
                    last = v.scalar_tensor_tensor(out=k, in0=val8[:, 0:VN], scalar=0.0, in1=k,
                                                  op0=ALU.is_gt, op1=ALU.mult)
                last.then_inc(S["masked_keys"], 1)
                hold(dve, S["masked_keys"], c + 1)
                sl, sh = slot_lo[:, 0:K].bitcast(F32), slot_hi[:, 0:K].bitcast(F32)
                R = K // 8
                for q in range(R):
                    s8 = slice(8 * q, 8 * q + 8)
                    v.max(sl[:, s8], kl)
                    v.max(sh[:, s8], kh).then_inc(S["sorted_"], 1)
                    hold(dve, S["sorted_"], j * (2 * R) + (rounds_before[ph] + 2 * q + 1))
                    if q < R - 1:
                        v.match_replace(kl, sl[:, s8], kl, 0.0)
                        v.match_replace(kh, sh[:, s8], kh, 0.0).then_inc(S["sorted_"], 1)
                    else:
                        v.tensor_scalar(jcol[:, 0:K], slot_lo[:, 0:K], JBITS, None, ALU.logical_shift_right
                                        ).then_inc(S["sorted_"], 1)
                    hold(dve, S["sorted_"], j * (2 * R) + (rounds_before[ph] + 2 * q + 2))
                v.tensor_scalar(far[:, 0:K], jcol[:, 0:K], 1.0, float(2 * N), ALU.is_lt, ALU.mult)
                v.tensor_scalar(off_mask[:, 0:K], jcol[:, 0:K], 1.0, NEG, ALU.is_lt, ALU.mult).then_inc(S["dec1"], 1)
                dve.wait_ge(S["dec1"], c + 1)
                if ph > 0 or not isinstance(j, int) or j >= 2:
                    pass
                v.tensor_tensor(offs[:, b, 0:K], jcol[:, 0:K], far[:, 0:K], ALU.add).then_inc(S["offs_ready"], 1)
                v.tensor_scalar(ahi[:, 0:K], slot_hi[:, 0:K], JBITS, 0x7FFFFFFF, ALU.logical_shift_left,
                                ALU.bitwise_and).then_inc(S["dec2"], 1)
                dve.wait_ge(S["dec2"], c + 1)
                v.scalar_tensor_tensor(out=aval[:, 0:K], in0=slot_lo[:, 0:K], scalar=LOW, in1=ahi[:, 0:K],
                                       op0=ALU.bitwise_and, op1=ALU.bitwise_or).then_inc(S["dec3"], 1)
                dve.wait_ge(S["flag_a"], c + 1)
                t = j + t0
                v.tensor_tensor(flags[:, bass.ds(t, 1)], flag8[:, :], sl[:, K - 1:K], ALU.max
                                ).then_inc(S["flag_b"], 1)
                dve.wait_ge(S["dec3"], c + 1)
                pv = pre[:, b, 0:K * H].rearrange("p (k h) -> p k h", h=H)
                v.tensor_tensor(pv, aval[:, 0:K].bitcast(F32).unsqueeze(2).to_broadcast([P, K, H]),
                                we_all[:, :].unsqueeze(1).to_broadcast([P, K, H]), ALU.mult).then_inc(S["az1"], 1)
                dve.wait_ge(S["az1"], c + 1)
                v.tensor_tensor(pv, pv, s_all[:, bass.ds(t, 1), :].to_broadcast([P, K, H]), ALU.add).then_inc(S["az2"], 1)
                dve.wait_ge(S["az2"], c + 1)
                v.tensor_tensor(pv, pv, off_mask[:, 0:K].unsqueeze(2).to_broadcast([P, K, H]), ALU.add
                                ).then_inc(S["pre_done"], 1)

            def edges(ph, j, b):
                t0, t1, K, NS = PHASES[ph]
                c = j + (t0 - FIRST)
                g0 = 0 if K > GSLOTS // 2 else b * (GSLOTS // 2)
                half = j // 2 if isinstance(j, int) else j >> 1
                dve.wait_ge(S[f"gath_in{b}"], half * (16 * K) + (bases[ph] + 16 * K))
                dve.wait_ge(S["pre_done"], c + 1)
                zv = z[:, 0:K * H].rearrange("p (k h) -> p k h", h=H)
                v.tensor_tensor(zv, pre[:, b, 0:K * H].rearrange("p (k h) -> p k h", h=H),
                                gath[:, g0:g0 + K, HD:ROW], ALU.add).then_inc(S["z1"], 1)
                dve.wait_ge(S["z1"], c + 1)
                v.scalar_tensor_tensor(out=z[:, 0:K * H], in0=z[:, 0:K * H], scalar=ALPHA, in1=z[:, 0:K * H],
                                       op0=ALU.mult, op1=ALU.max).then_inc(S["z2"], 1)
                dve.wait_ge(S["z2"], c + 1)
                zh = z[:, 0:K * H].rearrange("p (k h) -> p h k", h=H)
                v.tensor_reduce(rmax[:, :], zh, AX_X, ALU.max).then_inc(S["z3"], 1)
                dve.wait_ge(S["z3"], c + 1)
                v.tensor_tensor(zv, zv, rmax[:, :].unsqueeze(1).to_broadcast([P, K, H]), ALU.subtract
                                ).then_inc(S["z_ready"], 1)
                dve.wait_ge(S["exped"], c + 1)
                v.tensor_reduce(rsum[:, :], prob[:, 0:K * H].rearrange("p (k h) -> p h k", h=H), AX_X, ALU.add
                                ).then_inc(S["summed_p"], 1)
                dve.wait_ge(S["summed_p"], c + 1)
                v.reciprocal(rinv[:, :], rsum[:, :]).then_inc(S["recip"], 1)
                dve.wait_ge(S["recip"], c + 1)
                prv = prob[:, 0:K * H].rearrange("p (k h) -> p k h", h=H)
                v.tensor_tensor(prv, prv, rinv[:, :].unsqueeze(1).to_broadcast([P, K, H]), ALU.mult
                                ).then_inc(S["normed"], 1)
                dve.wait_ge(S["normed"], c + 1)
                for q in range(2):
                    ks = K // 2
                    gv = gath[:, g0 + q * ks:g0 + (q + 1) * ks, 0:HD].rearrange("p k (h d) -> p k h d", d=D)
                    pb = prob[:, q * ks * H:(q + 1) * ks * H].rearrange("p (k h) -> p k h", h=H)
                    v.tensor_tensor(gv, gv, pb.unsqueeze(3).to_broadcast([P, ks, H, D]), ALU.mult
                                    ).then_inc(S["weighted"], 1)

            scan(0, 0, 0)
            for ph, (t0, t1, K, NS) in enumerate(PHASES):
                n = t1 - t0
                if n > 2:
                    with dve.Fori(0, n // 2 - 1) as i:
                        scan(ph, 2 * i + 1, 1)
                        edges(ph, 2 * i, 0)
                        scan(ph, 2 * i + 2, 0)
                        edges(ph, 2 * i + 1, 1)
                scan(ph, n - 1, 1)
                edges(ph, n - 2, 0)
                if ph + 1 < len(PHASES):
                    scan(ph + 1, 0, 0)
                edges(ph, n - 1, 1)

            dve.wait_ge(S["fl_t"], 1)
            v.tensor_reduce(flagT[:, :], ps_flag[0:TILES, 0:P], AX_X, ALU.max).then_inc(S["fl_max"], 1)
            dve.wait_ge(S["fl_row"], 1)
            v.tensor_scalar(flag_row[:, :], ps_flag_row[0:1, 0:TILES], 0.0, None, ALU.is_gt).then_inc(S["fl_ready"], 1)

            done = dve.alloc_register("dense_dve")
            dve.reg_mov(done, 0)
            dve.wait_ge(S["fl_ready"], 1)
            with dve.Fori(0, TILES) as t:
                flag = dve.value_load(flag_row[0:1, bass.ds(t, 1)], min_val=0, max_val=1)
                with dve.If(flag > 0):
                    n = dve.snap(done)
                    dve.wait_ge(S["d_adj"], n * 16 + 16)
                    v.tensor_scalar(bias_m, a_t, 0.0, NEG, ALU.is_le, ALU.mult).then_inc(S["d_mask"], 1)
                    hold(dve, S["d_mask"], n + 1)

                    def finish(g, h, b):
                        dve.wait_ge(S["d_exp"], g + 1)
                        v.reciprocal(urec[:, b:b + 1], uden[:, b:b + 1]).then_inc(S["d_rec"], 1)
                        dve.wait_ge(S["d_rec"], g + 1)
                        dve.wait_ge(S["d_pv"], g + 3)
                        v.scalar_tensor_tensor(out=dout[:, bass.ts(h, D)], in0=ps_out[:, b, :],
                                               scalar=urec[:, b:b + 1], in1=dres[:, bass.ts(h, D)],
                                               op0=ALU.mult, op1=ALU.add).then_inc(S["d_fin"], 1)

                    def scores(g, h, b):
                        dve.wait_ge(S["d_dst"], g * 16 + 16)
                        dve.wait_ge(S["d_pv"], g + 1)
                        v.scalar_tensor_tensor(out=u_sb[b], in0=a_t, scalar=we_all[:, bass.ds(h, 1)], in1=dst_bc,
                                               op0=ALU.mult, op1=ALU.add).then_inc(S["d_u1"], 1)
                        hold(dve, S["d_u1"], g + 2)
                        v.tensor_tensor_reduce(u_sb[b], u_sb[b], bias_m, 1.0, -3e38, ALU.add, ALU.max,
                                               umax[:, b:b + 1]).then_inc(S["d_u2"], 1)
                        dve.wait_ge(S["d_u2"], g + 1)
                        v.tensor_tensor(ushift[:, b:b + 1], umax[:, b:b + 1],
                                        s_all[:, bass.ds(t, 1), bass.ds(h, 1)].rearrange("p a h -> p (a h)"),
                                        ALU.add).then_inc(S["d_m1"], 1)
                        dve.wait_ge(S["d_m1"], g + 1)
                        v.scalar_tensor_tensor(out=uleak[:, b:b + 1], in0=ushift[:, b:b + 1], scalar=ALPHA,
                                               in1=ushift[:, b:b + 1], op0=ALU.mult, op1=ALU.max
                                               ).then_inc(S["d_m2"], 1)
                        dve.wait_ge(S["d_m2"], g + 1)
                        v.tensor_scalar(nmax[:, b:b + 1], uleak[:, b:b + 1], -1.0, None, ALU.mult
                                        ).then_inc(S["d_m"], 1)

                    hold(dve, S["d_res"], n * 16 + 16)
                    with dve.Fori(0, H // 2) as hp:
                        for b in range(2):
                            scores(n * H + hp * 2 + b, hp * 2 + b, b)
                        for b in range(2):
                            g = n * H + hp * 2 + b
                            dve.wait_ge(S["d_src"], g + 1)
                            v.scalar_tensor_tensor(out=u_sb[b], in0=u_sb[b], scalar=ALPHA, in1=u_sb[b],
                                                   op0=ALU.mult, op1=ALU.max).then_inc(S["d_leak"], 1)
                        for b in range(2):
                            finish(n * H + hp * 2 + b, hp * 2 + b, b)
                    dve.reg_add(done, done, 1)

        @block.scalar
        def _(act):
            s = nc.scalar
            act.wait_ge(S["eps_set"], 1)
            def project(i):
                for b in range(2):
                    t = 2 * i + b
                    act.wait_ge(S["mv_done"], t + 1)
                    s.activation(sdev[:, b:b + 1], mv[:, 2 * b + 1:2 * b + 2], ACT.Sqrt, bias=eps[:, :]
                                 ).then_inc(S["sd_done"], 1)
                    act.wait_ge(S["hnT_ps"], t + 1)
                    s.activation(hnT[:, b, :], ps_hnT[:, b, :], ACT.Relu).then_inc(S["hnT_done"], 1)
                    act.wait_ge(S["proj_done"], t + 1)
                    if not isinstance(i, int):
                        act.wait_ge(S[f"hd_out{b}"], 16 * i)
                        act.wait_ge(S["s_done"], t - 1)
                    s.activation(hd_sb[:, b, :], ps_hd[:, b, :], ACT.Copy).then_inc(S["hd_copied"], 1)
                    if not isinstance(i, int):
                        act.wait_ge(S[f"dst_out{b}"], 16 * i)
                    s.activation(dst_sb[0:H, b, :], ps_dst[0:H, b, :], ACT.Copy).then_inc(S["dst_copied"], 1)

            project(0)
            with act.Fori(1, TILES // 2) as i:
                project(i)
            for b in range(2):
                act.wait_ge(S[f"res_out{b}"], 16 * (TILES // 2))

            def load_res(t, b):
                act.dma_start(res_sb[:, b, :], resid[bass.ts(t, P), :]).then_inc(S[f"res_in{b}"], 16)

            def tile(ph, j, b, i):
                t0, t1, K, NS = PHASES[ph]
                c = j + (t0 - FIRST)
                t = j + t0
                c2 = i + (t0 - FIRST) // 2
                act.wait_ge(S["z_ready"], c + 1)
                s.activation(prob[:, 0:K * H], z[:, 0:K * H], ACT.Exp).then_inc(S["exped"], 1)
                act.wait_ge(S["tile_sum"], c + 1)
                if not isinstance(c2, int) or c2:
                    act.wait_ge(S[f"out_st{b}"], c2 * 16)
                s.activation(out_sb[:, b, :], ps_sum[:, b, :], ACT.Copy).then_inc(S["out_copied"], 1)
                load_res(t + 2, b) if not (isinstance(t, int) and t + 2 >= TILES) else None
                act.wait_ge(S["out_copied"], c + 1)
                act.dma_start(out[bass.ts(t, P), :], out_sb[:, b, :]).then_inc(S[f"out_st{b}"], 16)

            load_res(FIRST, 0)
            load_res(FIRST + 1, 1)
            for ph, (t0, t1, K, NS) in enumerate(PHASES):
                pairs = (t1 - t0) // 2
                body = pairs - 1 if t1 == TILES else pairs
                if body == 1:
                    tile(ph, 0, 0, 0)
                    tile(ph, 1, 1, 0)
                else:
                    with act.Fori(0, body) as i:
                        for b in range(2):
                            tile(ph, 2 * i + b, b, i)
                if t1 == TILES:
                    for b in range(2):
                        tile(ph, 2 * (pairs - 1) + b, b, pairs - 1)
            for b in range(2):
                act.wait_ge(S[f"out_st{b}"], 16 * ((TILES - FIRST) // 2))

            done = act.alloc_register("dense_act")
            act.reg_mov(done, 0)
            act.wait_ge(S["fl_ready"], 1)
            with act.Fori(0, TILES) as t:
                flag = act.value_load(flag_row[0:1, bass.ds(t, 1)], min_val=0, max_val=1)
                with act.If(flag > 0):
                    n = act.snap(done)
                    with act.Fori(0, H // 2) as hp:
                        for b in range(2):
                            g = n * H + hp * 2 + b
                            h = hp * 2 + b
                            act.wait_ge(S["d_m"], g + 1)
                            s.activation(u_sb[b], u_sb[b], ACT.Identity,
                                         bias=s_all[:, bass.ds(t, 1), bass.ds(h, 1)].rearrange("p a h -> p (a h)")
                                         ).then_inc(S["d_src"], 1)
                        for b in range(2):
                            g = n * H + hp * 2 + b
                            act.wait_ge(S["d_leak"], g + 1)
                            s.activation(u_sb[b], u_sb[b], ACT.Exp, bias=nmax[:, b:b + 1],
                                         accum_out=uden[:, b:b + 1]).then_inc(S["d_exp"], 1)
                            for q in range(16):
                                act.wait_ge(S["d_tr"], g * 16 + (q + 1))
                                act.wait_ge(S["d_used"], g * 16 + (q + 1))
                                s.activation(pt_sb[:, q % 2, :], ps_pt[:, q % 2, :], ACT.Copy).then_inc(S["d_ev"], 1)
                    act.wait_ge(S["d_fin"], n * H + H)
                    act.dma_start(out[bass.ts(t, P), :], dout[:, :]).then_inc(S["d_out"], 16)
                    act.wait_ge(S["d_out"], n * 16 + 16)
                    act.sem_inc(S["d_free"], 1)
                    act.reg_add(done, done, 1)

        @block.tensor
        def _(pe):
            m = nc.tensor
            pe.wait_ge(S["ident_set"], 1)
            pe.wait_ge(S["w_in"], 32)
            pe.wait_ge(S["blk_in"], 16 * 16)
            for c in range(2):
                if c:
                    pe.wait_ge(S["wt_copied"], c)
                for q in range(2):
                    m.transpose(ps_w[:, q * P:(q + 1) * P], w_sb[:, q, c * P:(c + 1) * P], ident[:, :])
                    m.transpose(ps_w[:, HD + q * P:HD + (q + 1) * P], wr_sb[:, q, c * P:(c + 1) * P], ident[:, :])
                for q in range(2):
                    last = m.matmul(ps_w2[:, 0:16], w_sb[:, q, c * P:(c + 1) * P], a_blk[:, q, :],
                                    start=(q == 0), stop=(q == 1))
                last.then_inc(S["wt_done"], 1)
            pe.wait_ge(S["wt_copied"], 2)
            pe.wait_ge(S["small_in"], 48)
            with pe.Fori(0, TILES // 2) as i:
                for b in range(2):
                    t = 2 * i + b
                    pe.wait_ge(S["hn_done"], t + 1)
                    for c in range(2):
                        last = m.transpose(ps_hnT[:, b, c * P:(c + 1) * P], hn[:, b, c * P:(c + 1) * P], ident[:, :])
                    last.then_inc(S["hnT_ps"], 1)
                    pe.wait_ge(S["hnT_done"], t + 1)
                    for c in range(2):
                        m.matmul(ps_hd[:, b, :], hnT[:, b, c * P:(c + 1) * P], w_all[:, c, 0:272],
                                 start=(c == 0), stop=(c == 1))
                    for c in range(2):
                        m.matmul(ps_dst[0:H, b, :], w_all[:, c, HD:ROW], hnT[:, b, c * P:(c + 1) * P],
                                 start=(c == 0), stop=(c == 1))
                    for c in range(2):
                        m.matmul(ps_res[:, b, :], hnT[:, b, c * P:(c + 1) * P], w_all[:, c, 272:528],
                                 start=(c == 0), stop=False)
                    m.matmul(ps_res[:, b, :], ones[0:1, :], brow[:, :], start=False, stop=True
                             ).then_inc(S["proj_done"], 1)

            for ph, (t0, t1, K, NS) in enumerate(PHASES):
                with pe.Fori(0, (t1 - t0) // 2) as i:
                    for b in range(2):
                        c = 2 * i + (b + t0 - FIRST)
                        g0 = 0 if K > GSLOTS // 2 else b * (GSLOTS // 2)
                        pe.wait_ge(S[f"res_in{b}"], i * 16 + 16 * ((t0 - FIRST) // 2 + 1))
                        m.matmul(ps_sum[:, b, :], ident[:, :], res_sb[:, b, :], start=True, stop=False)
                        for k in range(K):
                            if k % (K // 2) == 0:
                                pe.wait_ge(S["weighted"], c * 2 + (k // (K // 2) + 1))
                            last = m.matmul(ps_sum[:, b, :], ident[:, :], gath[:, g0 + k, 0:HD],
                                            start=False, stop=(k == K - 1))
                        last.then_inc(S["tile_sum"], 1)

            pe.wait_ge(S["flag_b"], TILES - FIRST)
            m.transpose(ps_flag[0:TILES, 0:P], flags[:, :], ident[:, :]).then_inc(S["fl_t"], 1)
            pe.wait_ge(S["fl_max"], 1)
            m.matmul(ps_flag_row[0:1, 0:TILES], flagT[:, :], ident[0:TILES, 0:TILES], start=True, stop=True
                     ).then_inc(S["fl_row"], 1)

            pe.sem_inc(S["d_pv"], 2)
            pe.sem_inc(S["d_used"], 2)
            done = pe.alloc_register("dense_pe")
            pe.reg_mov(done, 0)
            pe.wait_ge(S["fl_ready"], 1)
            with pe.Fori(0, TILES) as t:
                flag = pe.value_load(flag_row[0:1, bass.ds(t, 1)], min_val=0, max_val=1)
                with pe.If(flag > 0):
                    n = pe.snap(done)
                    with pe.Fori(0, H // 2) as hp:
                        for b in range(2):
                            g = n * H + hp * 2 + b
                            pe.wait_ge(S["d_exp"], g + 1)
                            pe.wait_ge(S["d_h"], g * 16 + 16)
                            hv = h_sb[:, :].rearrange("p (c d) -> p c d", d=D)

                            def weighted(q):
                                pe.wait_ge(S["d_ev"], g * 16 + (q + 1))
                                for r in range(4):
                                    last = m.matmul(ps_out[:, b, :], pt_sb[:, q % 2, r * P:(r + 1) * P],
                                                    hv[:, 4 * q + r, :], start=(q == 0 and r == 0),
                                                    stop=(q == 15 and r == 3))
                                return last.then_inc(S["d_used"], 1)

                            for q in range(16):
                                for r in range(4):
                                    last = m.transpose(ps_pt[:, q % 2, r * P:(r + 1) * P],
                                                       u_sb[b][:, (4 * q + r) * P:(4 * q + r + 1) * P], ident[:, :])
                                last.then_inc(S["d_tr"], 1)
                                if q:
                                    weighted(q - 1)
                            weighted(15)
                            pe.wait_ge(S["d_used"], (g + 1) * 16 + 2)
                            pe.sem_inc(S["d_pv"], 1)
                    pe.reg_add(done, done, 1)


_INS = ["x", "adj", "L0_gnn_W", "L0_gnn_We", "L0_gnn_be", "L0_gnn_a_src", "L0_gnn_a_dst", "L0_gnn_Wr", "L0_gnn_br"]
_OUTS = [((N, HD), "float32")]


def kernel(**inputs):
    import numpy as _np
    import concourse.bacc as _bacc
    from concourse import mybir as _mybir
    from concourse.bass_utils import run_bass_kernel_spmd as _run

    nc = _bacc.Bacc("TRN2", target_bir_lowering=False, num_devices=1)
    arrays, args = {}, []
    for name in _INS:
        a = _np.ascontiguousarray(inputs[name])
        arrays[f"in_{name}_dram"] = a
        args.append(nc.dram_tensor(f"in_{name}_dram", a.shape, _mybir.dt.from_np(a.dtype), kind="ExternalInput").ap())
    for i, (shape, dtype) in enumerate(_OUTS):
        dt = _mybir.dt.from_np(_np.dtype(dtype))
        args.append(nc.dram_tensor(f"out_{i}_dram", shape, dt, kind="ExternalOutput").ap())
    gat_kernel(nc, *args)
    r = _run(nc, [arrays], core_ids=[0])
    got = tuple(r.results[0][f"out_{i}_dram"] for i in range(len(_OUTS)))
    return got[0]
```

```python
from contextlib import ExitStack

import numpy as np
import concourse.bass as bass
from concourse import mybir

ALU = mybir.AluOpType
ACT = mybir.ActivationFunctionType
F32 = mybir.dt.float32
U32 = mybir.dt.uint32
I32 = mybir.dt.int32
AX_X = mybir.AxisListType.X

P = 128
N = 8192
IN = 256
H = 8
D = 32
HD = H * D
TILES = N // P
UNITS = TILES // 2
ROW = HD + H
ALPHA = 0.2
EPS = 1e-5
NEG = -1e30
PAD = 64
JBITS = 17
LOW = (1 << JBITS) - 1
GSLOTS = 96

FIRST = 2
PHASES = [(2, 4, 64, 48), (4, 8, 56, 48), (8, 16, 40, 24), (16, 32, 32, 16), (32, 64, 24, 16)]
KMAX = max(p[2] for p in PHASES)
VMAX = 8 * max(p[3] for p in PHASES)


def segments(n):
    bounds = [0]
    for s in range(1, n + 1):
        bounds.append(max(bounds[-1] + 8, int(round(N * (s / n) ** 2))))
    return bounds


def gat_kernel(nc, x, adj, W, We, be, a_src, a_dst, Wr, br, out):
    table = nc.dram_tensor("table", (N + PAD, ROW), F32, kind="Internal").ap()
    resid = nc.dram_tensor("resid", (N, HD), F32, kind="Internal").ap()
    dst_rows = nc.dram_tensor("dst_rows", (H, N), F32, kind="Internal").ap()

    with ExitStack() as ctx:
        def sb(name, shape, dt=F32):
            return ctx.enter_context(nc.sbuf_tensor(name, shape, dt))

        def sem(name):
            return ctx.enter_context(nc.semaphore(name))

        banks = ctx.enter_context(nc.psum_tensor("banks", [P, 8, 512], F32))
        ps_hnT = banks[:, 0:2, :].rearrange("p u (b n) -> p u b n", b=2)
        ps_hd = banks[:, 2:6, 0:ROW + H].rearrange("p (u b) n -> p u b n", u=2)
        ps_dst = banks[:, 2:6, 384:512].rearrange("p (u b) n -> p u b n", u=2)
        ps_res = banks[:, 6:8, :].rearrange("p u (b n) -> p u b n", b=2)
        ps_w, ps_w2 = banks[:, 6, :], banks[:, 7, :]
        ps_sum = banks[:, 0:2, 0:HD]
        ps_pt = banks[:, 2:4, :]
        ps_out = banks[:, 4:6, 0:D]
        ps_flag, ps_flag_row = banks[:, 6, :], banks[:, 7, :]

        ident = sb("ident", [P, P])
        ones = sb("ones", [P, P])
        w_all = sb("w_all", [P, 2, 528])
        eps = sb("eps", [P, 1])
        brow = sb("brow", [1, HD])
        be_all = sb("be_all", [P, H])
        we_all = sb("we_all", [P, H])
        seg_base = {n: sb(f"seg_base{n}", [P, n * 8]) for n in sorted({p[3] for p in PHASES})}
        s_all = sb("s_all", [P, TILES, H])
        flags = sb("flags", [P, TILES])
        flagT = sb("flagT", [TILES, 1])
        flag_row = sb("flag_row", [1, TILES], I32)

        adj_sb = sb("adj_sb", [P, 2, N])
        gath = sb("gath", [P, GSLOTS, ROW])
        val8 = sb("val8", [P, VMAX])
        idx8 = sb("idx8", [P, VMAX], U32)
        jpad = sb("jpad", [P, VMAX], U32)
        key_lo = sb("key_lo", [P, VMAX], U32)
        key_hi = sb("key_hi", [P, VMAX], U32)
        slot_lo = sb("slot_lo", [P, KMAX], U32)
        slot_hi = sb("slot_hi", [P, KMAX], U32)
        jcol = sb("jcol", [P, KMAX], U32)
        far = sb("far", [P, KMAX])
        offs = sb("offs", [P, 2, KMAX], U32)
        aval = sb("aval", [P, KMAX], U32)
        ahi = sb("ahi", [P, KMAX], U32)
        off_mask = sb("off_mask", [P, KMAX])
        pre = sb("pre", [P, 2, KMAX * H])
        z = sb("z", [P, KMAX * H])
        prob = sb("prob", [P, KMAX * H])
        flag8 = sb("flag8", [P, 1])
        rmax = sb("rmax", [P, H])
        rsum = sb("rsum", [P, H])
        rinv = sb("rinv", [P, H])
        res_sb = sb("res_sb", [P, 2, HD])
        out_sb = sb("out_sb", [P, 2, HD])

        gflat = gath[:, :, :].rearrange("p k r -> p (k r)")
        at = [0]

        def part(width):
            at[0] += width
            return gflat[:, at[0] - width:at[0]]

        w_sb = part(2 * IN).rearrange("p (q n) -> p q n", q=2)
        wr_sb = part(2 * IN).rearrange("p (q n) -> p q n", q=2)
        a_blk = part(32).rearrange("p (q n) -> p q n", q=2)
        x_sb = part(4 * 2 * IN).rearrange("p (u b n) -> p u b n", u=4, b=2)
        hn = part(2 * 2 * IN).rearrange("p (u b n) -> p u b n", u=2, b=2)
        hnT = part(2 * 2 * IN).rearrange("p (u b n) -> p u b n", u=2, b=2)
        hd_sb = part(2 * 2 * (ROW + H)).rearrange("p (u b n) -> p u b n", u=2, b=2)
        rt_sb = part(2 * 2 * HD).rearrange("p (u b n) -> p u b n", u=2, b=2)
        dst_sb = part(2 * 2 * P).rearrange("p (u b n) -> p u b n", u=2, b=2)
        stat = part(4 * 12).rearrange("p (u b n) -> p u b n", u=4, b=2)
        mv = part(4 * 4).rearrange("p (u b n) -> p u b n", u=4, b=2)
        rstd = part(4 * 2).rearrange("p (u b) -> p u b", u=4)
        sdev = part(4 * 2).rearrange("p (u b) -> p u b", u=4)
        assert at[0] <= GSLOTS * ROW
        bias_m = gflat[:, 0:N]
        dst_bc = gflat[:, N:2 * N]
        u_sb = [adj_sb[:, 1, :], gflat[:, 2 * N:3 * N]]
        a_t = adj_sb[:, 0, :]
        pt_sb = pre[:, :, 0:512]
        h_sb = sb("h_sb", [P, TILES * D])
        umax = sb("umax", [P, 2])
        ushift = sb("ushift", [P, 2])
        uleak = sb("uleak", [P, 2])
        nmax = sb("nmax", [P, 2])
        uden = sb("uden", [P, 2])
        urec = sb("urec", [P, 2])
        dres = sb("dres", [P, HD])
        dout = sb("dout", [P, HD])

        S = {n: sem(n) for n in (
            "ones_set", "held", "ident_set", "blk_zero", "blk_in", "w_in", "small_in", "wt_done", "wt_copied",
            "x_in0", "x_in1", "x_in2", "x_in3", "x_free", "bn_done", "mv_done", "sd_done", "eps_set", "rstd_done", "hn_done", "hnT_ps", "hnT_done",
            "proj_done", "hd_copied", "dst_copied", "s_done", "res_done",
            "hd_out0", "hd_out1", "res_out0", "res_out1", "dst_out0", "dst_out1", "gath_zero", "pad_out", "base_set",
            "adj_in0", "adj_in1", "maxed", "scanned", "jadd", "jshift", "keyed", "masked_keys", "sorted_",
            "dec1", "dec2", "dec3", "decoded", "az1", "az2", "pre_done", "offs_ready", "flag_a", "flag_b",
            "gath_in0", "gath_in1", "z1", "z2", "z3", "z_ready", "exped", "summed_p", "recip", "normed",
            "weighted", "tile_sum", "out_copied", "out_st0", "out_st1", "res_in0", "res_in1",
            "fl_t", "fl_max", "fl_row", "fl_ready", "flag_init",
            "d_adj", "d_free", "d_mask", "d_dst", "d_h", "d_u1", "d_u2", "d_m1", "d_m2", "d_m", "d_leak", "d_src", "d_exp",
            "d_tr", "d_ev", "d_used", "d_pv", "d_rec", "d_fin", "d_res", "d_out")}

        def hold(eng, semaphore, value):
            eng.wait_ge(semaphore, value)
            eng.sem_inc(S["held"], 1)

        load_adj = lambda t: adj[bass.ts(t, P), :]
        by_unit = lambda a, u: a[bass.ts(u, 2 * P), :].rearrange("(b p) n -> p b n", p=P)
        block = ctx.enter_context(nc.Block())

        @block.sync
        def _(sp):
            sp.dma_start(w_sb, W.rearrange("(q p) n -> p q n", p=P)).then_inc(S["w_in"], 16)
            sp.dma_start(wr_sb, Wr.rearrange("(q p) n -> p q n", p=P)).then_inc(S["w_in"], 16)
            sp.dma_start(brow[:, :], br.rearrange("(a n) -> a n", a=1)).then_inc(S["small_in"], 16)
            sp.dma_start(be_all[:, :], be.partition_broadcast(P)).then_inc(S["small_in"], 16)
            sp.dma_start(we_all[:, :], We.rearrange("h a -> (h a)").partition_broadcast(P)).then_inc(S["small_in"], 16)
            sp.wait_ge(S["blk_zero"], 1)
            for q in range(2):
                for r in range(4):
                    h = 4 * q + r
                    for o, a in ((0, a_dst), (H, a_src)):
                        sp.dma_start(a_blk[D * r:D * r + D, q, o + h:o + h + 1],
                                     a[h, :].rearrange("(d a) -> d a", a=1)).then_inc(S["blk_in"], 16)
            with sp.Fori(0, UNITS // 4) as i:
                for q in range(4):
                    u = 4 * i + q
                    sp.wait_ge(S["x_free"], u + 1)
                    sp.dma_start(x_sb[:, q, :, :], by_unit(x, u)).then_inc(S[f"x_in{q}"], 16)
            c = 0
            for t0, t1, K, NS in PHASES:
                def load(t, c, b):
                    sp.dma_start(adj_sb[:, b, :], load_adj(t)).then_inc(S[f"adj_in{b}"], 16)
                if t0 == FIRST:
                    for t in range(t0, t1):
                        if c >= 2:
                            sp.wait_ge(S["scanned"], c - 1)
                        load(t, c, t % 2)
                        c += 1
                else:
                    with sp.Fori(0, (t1 - t0) // 2) as i:
                        for b in range(2):
                            sp.wait_ge(S["scanned"], 2 * i + (c + b - 1))
                            load(2 * i + (t0 + b), c, b)
                    c += t1 - t0
            sp.sem_inc(S["d_free"], 1)
            sp.sem_inc(S["d_u1"], 1)
            done = sp.alloc_register("dense_sp")
            sp.reg_mov(done, 0)
            sp.wait_ge(S["fl_ready"], 1)
            with sp.Fori(0, TILES) as t:
                flag = sp.value_load(flag_row[0:1, bass.ds(t, 1)], min_val=0, max_val=1)
                with sp.If(flag > 0):
                    n = sp.snap(done)
                    sp.wait_ge(S["d_free"], n + 1)
                    sp.dma_start(a_t, load_adj(t)).then_inc(S["d_adj"], 16)
                    sp.dma_start(dres[:, :], resid[bass.ts(t, P), :]).then_inc(S["d_res"], 16)
                    with sp.Fori(0, H // 2) as hp:
                        for b in range(2):
                            g = n * H + hp * 2 + b
                            h = hp * 2 + b
                            sp.wait_ge(S["d_u1"], g + 1)
                            sp.dma_start(dst_bc, dst_rows[bass.ds(h, 1), :].partition_broadcast(P)[:, 0, :]).then_inc(S["d_dst"], 16)
                            sp.wait_ge(S["d_pv"], g + 2)
                            sp.dma_start(h_sb[:, :].rearrange("p (c d) -> p c d", d=D),
                                         table[PAD:, :].rearrange("(c p) r -> p c r", p=P)[:, :, bass.ts(h, D)]
                                         ).then_inc(S["d_h"], 16)
                    sp.reg_add(done, done, 1)

        @block.gpsimd
        def _(pool):
            pool.memset(ones[:, :], 1.0).then_inc(S["ones_set"], 1)
            pool.memset(eps[:, :], EPS).then_inc(S["eps_set"], 1)
            pool.memset(a_blk, 0.0).then_inc(S["blk_zero"], 1)
            pool.memset(flags[:, :], 1.0).then_inc(S["flag_init"], 1)
            for n, base in seg_base.items():
                bounds = segments(n)
                for s in range(n):
                    last = pool.memset(base[:, 8 * s:8 * s + 8], float(bounds[s] + PAD))
            last.then_inc(S["base_set"], 1)
            pool.wait_ge(S["ones_set"], 1)
            pool.affine_select(out=ident[:, :], in_=ones[:, :], compare_op=ALU.is_equal, fill=0.0,
                               base=0, pattern=[[-1, P]], channel_multiplier=1).then_inc(S["ident_set"], 1)
            with pool.Fori(0, UNITS // 2) as i:
                for q in range(2):
                    u = 2 * i + q
                    pool.wait_ge(S["hd_copied"], u + 1)
                    pool.dma_start(by_unit(table[PAD:, :], u), hd_sb[:, q, :, 0:ROW]).then_inc(S[f"hd_out{q}"], 16)
                    pool.wait_ge(S["dst_copied"], u + 1)
                    pool.dma_start(dst_rows[:, bass.ts(u, 2 * P)].rearrange("h (b p) -> h b p", b=2),
                                   dst_sb[0:H, q, :, :]).then_inc(S[f"dst_out{q}"], 16)
                    pool.wait_ge(S["res_done"], u + 1)
                    pool.dma_start(by_unit(resid, u), rt_sb[:, q, :, :]).then_inc(S[f"res_out{q}"], 16)
            for b in range(2):
                for q in ("hd_out", "dst_out", "res_out"):
                    pool.wait_ge(S[f"{q}{b}"], 16 * (UNITS // 2))
            pool.memset(gflat, 0.0).then_inc(S["gath_zero"], 1)
            pool.wait_ge(S["gath_zero"], 1)
            pool.dma_start(table[0:PAD, :], gath[0:PAD, 0, :]).then_inc(S["pad_out"], 16)
            pool.wait_ge(S["pad_out"], 16)
            c = 0
            single = False
            for t0, t1, K, NS in PHASES:
                if single and K <= GSLOTS // 2:
                    pool.wait_ge(S["tile_sum"], c)
                single = K > GSLOTS // 2

                def gather(i):
                    for b in range(2):
                        if not isinstance(i, int) or c + b:
                            pool.wait_ge(S["tile_sum"], 2 * i + (c + b - (0 if single else 1)))
                        hold(pool, S["offs_ready"], 2 * i + (c + b + 1))
                        g0 = 0 if single else b * (GSLOTS // 2)
                        for k in range(K):
                            pool.indirect_dma_start(
                                gath[:, g0 + k, :], None, table[:, :],
                                bass.IndirectOffsetOnAxis(ap=offs[:, b, k:k + 1], axis=0),
                                bounds_check=N + PAD - 1, oob_is_err=False).then_inc(S[f"gath_in{b}"], 16)

                if t1 - t0 == 2:
                    gather(0)
                else:
                    with pool.Fori(0, (t1 - t0) // 2) as i:
                        gather(i)
                c += t1 - t0

        def gather_counts():
            base, at = [], 0
            for t0, t1, K, NS in PHASES:
                base.append(at)
                at += (t1 - t0) // 2 * 16 * K
            return base

        @block.vector
        def _(dve):
            v = nc.vector
            for c in range(2):
                dve.wait_ge(S["wt_done"], c + 1)
                v.tensor_copy(w_all[:, c, 0:HD], ps_w[:, 0:HD])
                v.tensor_copy(w_all[:, c, 272:528], ps_w[:, HD:2 * HD])
                v.tensor_copy(w_all[:, c, HD:HD + 16], ps_w2[:, 0:16]).then_inc(S["wt_copied"], 1)
            dve.sem_inc(S["x_free"], 4)
            dve.wait_ge(S["small_in"], 48)

            def normalize(u, q):
                i = u // 4 if isinstance(u, int) else u >> 2
                dve.wait_ge(S[f"x_in{q}"], 16 * i + 16)
                for b in range(2):
                    last = v.bn_stats(stat[:, q, b, :], x_sb[:, q, b, :])
                last.then_inc(S["bn_done"], 1)
                hold(dve, S["bn_done"], u + 1)
                for b in range(2):
                    last = v.bn_aggr(mv[:, q, b, :], stat[:, q, b, :])
                last.then_inc(S["mv_done"], 1)
                dve.wait_ge(S["sd_done"], u + 1)
                v.reciprocal(rstd[:, q, :], sdev[:, q, :]).then_inc(S["rstd_done"], 1)
                dve.wait_ge(S["rstd_done"], u + 1)
                if not isinstance(u, int) or u >= 2:
                    dve.wait_ge(S["hnT_ps"], u - 1)
                for b in range(2):
                    last = v.tensor_scalar(hn[:, q % 2, b, :], x_sb[:, q, b, :], mv[:, q, b, 0:1],
                                           rstd[:, q, b:b + 1], ALU.subtract, ALU.mult)
                last.then_inc(S["hn_done"], 1)

            def add_biases(u, q):
                dve.wait_ge(S["hd_copied"], u + 1)
                v.tensor_tensor(s_all[:, bass.ts(u, 2), :], hd_sb[:, q % 2, :, ROW:ROW + H],
                                be_all[:, :].unsqueeze(1).to_broadcast([P, 2, H]), ALU.add).then_inc(S["s_done"], 1)
                if not isinstance(u, int):
                    dve.wait_ge(S[f"res_out{q % 2}"], (u >> 1) * 16)
                elif u >= 2:
                    dve.wait_ge(S[f"res_out{q % 2}"], u // 2 * 16)
                v.tensor_tensor(rt_sb[:, q % 2, :, :], ps_res[:, q % 2, :, :], x_sb[:, q, :, :], ALU.add
                                ).then_inc(S["res_done"], 1)
                hold(dve, S["res_done"], u + 1)
                dve.sem_inc(S["x_free"], 1)

            for u in range(4):
                normalize(u, u % 4)
                if u >= 2:
                    add_biases(u - 2, (u - 2) % 4)
            with dve.Fori(1, UNITS // 4) as i:
                for q in range(4):
                    normalize(4 * i + q, q)
                    add_biases(4 * i + (q - 2), (q - 2) % 4)
            for u in range(UNITS - 2, UNITS):
                add_biases(u, u % 4)

            dve.wait_ge(S["base_set"], 1)
            dve.wait_ge(S["flag_init"], 1)
            dve.wait_ge(S["s_done"], UNITS)
            bases = gather_counts()
            rounds_before = []
            r = 0
            for t0, t1, K, NS in PHASES:
                rounds_before.append(r)
                r += (t1 - t0) * (2 * (K // 8))

            def scan(ph, j, b):
                t0, t1, K, NS = PHASES[ph]
                c = j + (t0 - FIRST)
                VN = 8 * NS
                bounds = segments(NS)
                hold(dve, S[f"adj_in{b}"], (c // 2 if isinstance(c, int) else c >> 1) * 16 + 16)
                a = adj_sb[:, b, :]
                for s in range(NS):
                    last = v.max(val8[:, 8 * s:8 * s + 8], a[:, bounds[s]:bounds[s + 1]])
                last.then_inc(S["maxed"], 1)
                hold(dve, S["maxed"], c + 1)
                for s in range(NS):
                    last = v.max_index(idx8[:, 8 * s:8 * s + 8], val8[:, 8 * s:8 * s + 8],
                                       a[:, bounds[s]:bounds[s + 1]])
                last.then_inc(S["scanned"], 1)
                v.tensor_reduce(flag8[:, :], val8[:, 0:VN].rearrange("p (s e) -> p s e", e=8)[:, :, 7],
                                AX_X, ALU.max).then_inc(S["flag_a"], 1)
                dve.wait_ge(S["scanned"], c + 1)
                v.tensor_tensor(jpad[:, 0:VN], idx8[:, 0:VN], seg_base[NS][:, :], ALU.add).then_inc(S["jadd"], 1)
                dve.wait_ge(S["jadd"], c + 1)
                v.tensor_scalar(idx8[:, 0:VN], jpad[:, 0:VN], JBITS, None, ALU.logical_shift_left
                                ).then_inc(S["jshift"], 1)
                dve.wait_ge(S["jshift"], c + 1)
                vb = val8[:, 0:VN].bitcast(U32)
                v.scalar_tensor_tensor(out=key_lo[:, 0:VN], in0=vb, scalar=LOW, in1=idx8[:, 0:VN],
                                       op0=ALU.bitwise_and, op1=ALU.bitwise_or)
                v.scalar_tensor_tensor(out=key_hi[:, 0:VN], in0=vb, scalar=JBITS, in1=idx8[:, 0:VN],
                                       op0=ALU.logical_shift_right, op1=ALU.bitwise_or).then_inc(S["keyed"], 1)
                dve.wait_ge(S["keyed"], c + 1)
                kl, kh = key_lo[:, 0:VN].bitcast(F32), key_hi[:, 0:VN].bitcast(F32)
                for k in (kl, kh):
                    last = v.scalar_tensor_tensor(out=k, in0=val8[:, 0:VN], scalar=0.0, in1=k,
                                                  op0=ALU.is_gt, op1=ALU.mult)
                last.then_inc(S["masked_keys"], 1)
                hold(dve, S["masked_keys"], c + 1)
                sl, sh = slot_lo[:, 0:K].bitcast(F32), slot_hi[:, 0:K].bitcast(F32)
                R = K // 8
                for q in range(R):
                    s8 = slice(8 * q, 8 * q + 8)
                    v.max(sl[:, s8], kl)
                    v.max(sh[:, s8], kh).then_inc(S["sorted_"], 1)
                    hold(dve, S["sorted_"], j * (2 * R) + (rounds_before[ph] + 2 * q + 1))
                    if q < R - 1:
                        v.match_replace(kl, sl[:, s8], kl, 0.0)
                        v.match_replace(kh, sh[:, s8], kh, 0.0).then_inc(S["sorted_"], 1)
                    else:
                        v.tensor_scalar(jcol[:, 0:K], slot_lo[:, 0:K], JBITS, None, ALU.logical_shift_right
                                        ).then_inc(S["sorted_"], 1)
                    hold(dve, S["sorted_"], j * (2 * R) + (rounds_before[ph] + 2 * q + 2))
                v.tensor_scalar(far[:, 0:K], jcol[:, 0:K], 1.0, float(2 * N), ALU.is_lt, ALU.mult)
                v.tensor_scalar(off_mask[:, 0:K], jcol[:, 0:K], 1.0, NEG, ALU.is_lt, ALU.mult).then_inc(S["dec1"], 1)
                dve.wait_ge(S["dec1"], c + 1)
                if ph > 0 or not isinstance(j, int) or j >= 2:
                    pass
                v.tensor_tensor(offs[:, b, 0:K], jcol[:, 0:K], far[:, 0:K], ALU.add).then_inc(S["offs_ready"], 1)
                v.tensor_scalar(ahi[:, 0:K], slot_hi[:, 0:K], JBITS, 0x7FFFFFFF, ALU.logical_shift_left,
                                ALU.bitwise_and).then_inc(S["dec2"], 1)
                dve.wait_ge(S["dec2"], c + 1)
                v.scalar_tensor_tensor(out=aval[:, 0:K], in0=slot_lo[:, 0:K], scalar=LOW, in1=ahi[:, 0:K],
                                       op0=ALU.bitwise_and, op1=ALU.bitwise_or).then_inc(S["dec3"], 1)
                dve.wait_ge(S["flag_a"], c + 1)
                t = j + t0
                v.tensor_tensor(flags[:, bass.ds(t, 1)], flag8[:, :], sl[:, K - 1:K], ALU.max
                                ).then_inc(S["flag_b"], 1)
                dve.wait_ge(S["dec3"], c + 1)
                pv = pre[:, b, 0:K * H].rearrange("p (k h) -> p k h", h=H)
                v.tensor_tensor(pv, aval[:, 0:K].bitcast(F32).unsqueeze(2).to_broadcast([P, K, H]),
                                we_all[:, :].unsqueeze(1).to_broadcast([P, K, H]), ALU.mult).then_inc(S["az1"], 1)
                dve.wait_ge(S["az1"], c + 1)
                v.tensor_tensor(pv, pv, s_all[:, bass.ds(t, 1), :].to_broadcast([P, K, H]), ALU.add).then_inc(S["az2"], 1)
                dve.wait_ge(S["az2"], c + 1)
                v.tensor_tensor(pv, pv, off_mask[:, 0:K].unsqueeze(2).to_broadcast([P, K, H]), ALU.add
                                ).then_inc(S["pre_done"], 1)

            def edges(ph, j, b):
                t0, t1, K, NS = PHASES[ph]
                c = j + (t0 - FIRST)
                g0 = 0 if K > GSLOTS // 2 else b * (GSLOTS // 2)
                half = j // 2 if isinstance(j, int) else j >> 1
                dve.wait_ge(S[f"gath_in{b}"], half * (16 * K) + (bases[ph] + 16 * K))
                dve.wait_ge(S["pre_done"], c + 1)
                zv = z[:, 0:K * H].rearrange("p (k h) -> p k h", h=H)
                v.tensor_tensor(zv, pre[:, b, 0:K * H].rearrange("p (k h) -> p k h", h=H),
                                gath[:, g0:g0 + K, HD:ROW], ALU.add).then_inc(S["z1"], 1)
                dve.wait_ge(S["z1"], c + 1)
                v.scalar_tensor_tensor(out=z[:, 0:K * H], in0=z[:, 0:K * H], scalar=ALPHA, in1=z[:, 0:K * H],
                                       op0=ALU.mult, op1=ALU.max).then_inc(S["z2"], 1)
                dve.wait_ge(S["z2"], c + 1)
                zh = z[:, 0:K * H].rearrange("p (k h) -> p h k", h=H)
                v.tensor_reduce(rmax[:, :], zh, AX_X, ALU.max).then_inc(S["z3"], 1)
                dve.wait_ge(S["z3"], c + 1)
                v.tensor_tensor(zv, zv, rmax[:, :].unsqueeze(1).to_broadcast([P, K, H]), ALU.subtract
                                ).then_inc(S["z_ready"], 1)
                dve.wait_ge(S["exped"], c + 1)
                v.tensor_reduce(rsum[:, :], prob[:, 0:K * H].rearrange("p (k h) -> p h k", h=H), AX_X, ALU.add
                                ).then_inc(S["summed_p"], 1)
                dve.wait_ge(S["summed_p"], c + 1)
                v.reciprocal(rinv[:, :], rsum[:, :]).then_inc(S["recip"], 1)
                dve.wait_ge(S["recip"], c + 1)
                prv = prob[:, 0:K * H].rearrange("p (k h) -> p k h", h=H)
                v.tensor_tensor(prv, prv, rinv[:, :].unsqueeze(1).to_broadcast([P, K, H]), ALU.mult
                                ).then_inc(S["normed"], 1)
                dve.wait_ge(S["normed"], c + 1)
                for q in range(2):
                    ks = K // 2
                    gv = gath[:, g0 + q * ks:g0 + (q + 1) * ks, 0:HD].rearrange("p k (h d) -> p k h d", d=D)
                    pb = prob[:, q * ks * H:(q + 1) * ks * H].rearrange("p (k h) -> p k h", h=H)
                    v.tensor_tensor(gv, gv, pb.unsqueeze(3).to_broadcast([P, ks, H, D]), ALU.mult
                                    ).then_inc(S["weighted"], 1)

            scan(0, 0, 0)
            for ph, (t0, t1, K, NS) in enumerate(PHASES):
                n = t1 - t0
                if n > 2:
                    with dve.Fori(0, n // 2 - 1) as i:
                        scan(ph, 2 * i + 1, 1)
                        edges(ph, 2 * i, 0)
                        scan(ph, 2 * i + 2, 0)
                        edges(ph, 2 * i + 1, 1)
                scan(ph, n - 1, 1)
                edges(ph, n - 2, 0)
                if ph + 1 < len(PHASES):
                    scan(ph + 1, 0, 0)
                edges(ph, n - 1, 1)

            dve.wait_ge(S["fl_t"], 1)
            v.tensor_reduce(flagT[:, :], ps_flag[0:TILES, 0:P], AX_X, ALU.max).then_inc(S["fl_max"], 1)
            dve.wait_ge(S["fl_row"], 1)
            v.tensor_scalar(flag_row[:, :], ps_flag_row[0:1, 0:TILES], 0.0, None, ALU.is_gt).then_inc(S["fl_ready"], 1)

            done = dve.alloc_register("dense_dve")
            dve.reg_mov(done, 0)
            dve.wait_ge(S["fl_ready"], 1)
            with dve.Fori(0, TILES) as t:
                flag = dve.value_load(flag_row[0:1, bass.ds(t, 1)], min_val=0, max_val=1)
                with dve.If(flag > 0):
                    n = dve.snap(done)
                    dve.wait_ge(S["d_adj"], n * 16 + 16)
                    v.tensor_scalar(bias_m, a_t, 0.0, NEG, ALU.is_le, ALU.mult).then_inc(S["d_mask"], 1)
                    hold(dve, S["d_mask"], n + 1)

                    def finish(g, h, b):
                        dve.wait_ge(S["d_exp"], g + 1)
                        v.reciprocal(urec[:, b:b + 1], uden[:, b:b + 1]).then_inc(S["d_rec"], 1)
                        dve.wait_ge(S["d_rec"], g + 1)
                        dve.wait_ge(S["d_pv"], g + 3)
                        v.scalar_tensor_tensor(out=dout[:, bass.ts(h, D)], in0=ps_out[:, b, :],
                                               scalar=urec[:, b:b + 1], in1=dres[:, bass.ts(h, D)],
                                               op0=ALU.mult, op1=ALU.add).then_inc(S["d_fin"], 1)

                    def scores(g, h, b):
                        dve.wait_ge(S["d_dst"], g * 16 + 16)
                        dve.wait_ge(S["d_pv"], g + 1)
                        v.scalar_tensor_tensor(out=u_sb[b], in0=a_t, scalar=we_all[:, bass.ds(h, 1)], in1=dst_bc,
                                               op0=ALU.mult, op1=ALU.add).then_inc(S["d_u1"], 1)
                        hold(dve, S["d_u1"], g + 2)
                        v.tensor_tensor_reduce(u_sb[b], u_sb[b], bias_m, 1.0, -3e38, ALU.add, ALU.max,
                                               umax[:, b:b + 1]).then_inc(S["d_u2"], 1)
                        dve.wait_ge(S["d_u2"], g + 1)
                        v.tensor_tensor(ushift[:, b:b + 1], umax[:, b:b + 1],
                                        s_all[:, bass.ds(t, 1), bass.ds(h, 1)].rearrange("p a h -> p (a h)"),
                                        ALU.add).then_inc(S["d_m1"], 1)
                        dve.wait_ge(S["d_m1"], g + 1)
                        v.scalar_tensor_tensor(out=uleak[:, b:b + 1], in0=ushift[:, b:b + 1], scalar=ALPHA,
                                               in1=ushift[:, b:b + 1], op0=ALU.mult, op1=ALU.max
                                               ).then_inc(S["d_m2"], 1)
                        dve.wait_ge(S["d_m2"], g + 1)
                        v.tensor_scalar(nmax[:, b:b + 1], uleak[:, b:b + 1], -1.0, None, ALU.mult
                                        ).then_inc(S["d_m"], 1)

                    hold(dve, S["d_res"], n * 16 + 16)

                    def leak(g, h, b):
                        dve.wait_ge(S["d_src"], g + 1)
                        v.scalar_tensor_tensor(out=u_sb[b], in0=u_sb[b], scalar=ALPHA, in1=u_sb[b],
                                               op0=ALU.mult, op1=ALU.max).then_inc(S["d_leak"], 1)

                    G = n * H
                    scores(G, 0, 0)
                    leak(G, 0, 0)
                    with dve.Fori(0, H // 2 - 1) as hp:
                        h = hp * 2
                        scores(G + h + 1, h + 1, 1)
                        leak(G + h + 1, h + 1, 1)
                        finish(G + h, h, 0)
                        scores(G + h + 2, h + 2, 0)
                        leak(G + h + 2, h + 2, 0)
                        finish(G + h + 1, h + 1, 1)
                    scores(G + 7, 7, 1)
                    leak(G + 7, 7, 1)
                    finish(G + 6, 6, 0)
                    finish(G + 7, 7, 1)
                    dve.reg_add(done, done, 1)

        @block.scalar
        def _(act):
            s = nc.scalar
            act.wait_ge(S["eps_set"], 1)
            def deviation(u, q):
                act.wait_ge(S["mv_done"], u + 1)
                s.activation(sdev[:, q, :], mv[:, q, :, 1], ACT.Sqrt, bias=eps[:, :]).then_inc(S["sd_done"], 1)

            def relu(u, q):
                act.wait_ge(S["hnT_ps"], u + 1)
                s.activation(hnT[:, q % 2, :, :], ps_hnT[:, q % 2, :, :], ACT.Relu).then_inc(S["hnT_done"], 1)

            def copies(u, q):
                act.wait_ge(S["proj_done"], u + 1)
                if not isinstance(u, int) or u >= 2:
                    half = u // 2 if isinstance(u, int) else u >> 1
                    act.wait_ge(S[f"hd_out{q % 2}"], half * 16)
                    act.wait_ge(S[f"dst_out{q % 2}"], half * 16)
                    act.wait_ge(S["s_done"], u - 1)
                s.activation(hd_sb[:, q % 2, :, :], ps_hd[:, q % 2, :, :], ACT.Copy).then_inc(S["hd_copied"], 1)
                s.activation(dst_sb[0:H, q % 2, :, :], ps_dst[0:H, q % 2, :, :], ACT.Copy).then_inc(S["dst_copied"], 1)

            deviation(0, 0)
            deviation(1, 1)
            relu(0, 0)
            deviation(2, 2)
            relu(1, 1)
            copies(0, 0)
            with act.Fori(0, UNITS // 4 - 1) as i:
                for q in range(4):
                    deviation(4 * i + (q + 3), (q + 3) % 4)
                    relu(4 * i + (q + 2), (q + 2) % 4)
                    copies(4 * i + (q + 1), (q + 1) % 4)
            deviation(UNITS - 1, 3)
            relu(UNITS - 2, 2)
            copies(UNITS - 3, 1)
            relu(UNITS - 1, 3)
            copies(UNITS - 2, 2)
            copies(UNITS - 1, 3)
            for b in range(2):
                act.wait_ge(S[f"res_out{b}"], 16 * (UNITS // 2))

            def load_res(t, b):
                act.dma_start(res_sb[:, b, :], resid[bass.ts(t, P), :]).then_inc(S[f"res_in{b}"], 16)

            def tile(ph, j, b, i):
                t0, t1, K, NS = PHASES[ph]
                c = j + (t0 - FIRST)
                t = j + t0
                c2 = i + (t0 - FIRST) // 2
                act.wait_ge(S["z_ready"], c + 1)
                s.activation(prob[:, 0:K * H], z[:, 0:K * H], ACT.Exp).then_inc(S["exped"], 1)
                act.wait_ge(S["tile_sum"], c + 1)
                if not isinstance(c2, int) or c2:
                    act.wait_ge(S[f"out_st{b}"], c2 * 16)
                s.activation(out_sb[:, b, :], ps_sum[:, b, :], ACT.Copy).then_inc(S["out_copied"], 1)
                load_res(t + 2, b) if not (isinstance(t, int) and t + 2 >= TILES) else None
                act.wait_ge(S["out_copied"], c + 1)
                act.dma_start(out[bass.ts(t, P), :], out_sb[:, b, :]).then_inc(S[f"out_st{b}"], 16)

            load_res(FIRST, 0)
            load_res(FIRST + 1, 1)
            for ph, (t0, t1, K, NS) in enumerate(PHASES):
                pairs = (t1 - t0) // 2
                body = pairs - 1 if t1 == TILES else pairs
                if body == 1:
                    tile(ph, 0, 0, 0)
                    tile(ph, 1, 1, 0)
                else:
                    with act.Fori(0, body) as i:
                        for b in range(2):
                            tile(ph, 2 * i + b, b, i)
                if t1 == TILES:
                    for b in range(2):
                        tile(ph, 2 * (pairs - 1) + b, b, pairs - 1)
            for b in range(2):
                act.wait_ge(S[f"out_st{b}"], 16 * ((TILES - FIRST) // 2))

            done = act.alloc_register("dense_act")
            act.reg_mov(done, 0)
            act.wait_ge(S["fl_ready"], 1)
            with act.Fori(0, TILES) as t:
                flag = act.value_load(flag_row[0:1, bass.ds(t, 1)], min_val=0, max_val=1)
                with act.If(flag > 0):
                    n = act.snap(done)

                    def add_source(g, h, b):
                        act.wait_ge(S["d_m"], g + 1)
                        s.activation(u_sb[b], u_sb[b], ACT.Identity,
                                     bias=s_all[:, bass.ds(t, 1), bass.ds(h, 1)].rearrange("p a h -> p (a h)")
                                     ).then_inc(S["d_src"], 1)

                    def head(g, h, b, last):
                        act.wait_ge(S["d_leak"], g + 1)
                        s.activation(u_sb[b], u_sb[b], ACT.Exp, bias=nmax[:, b:b + 1],
                                     accum_out=uden[:, b:b + 1]).then_inc(S["d_exp"], 1)
                        for q in range(16):
                            if q == 10 and not last:
                                add_source(g + 1, h + 1, 1 - b)
                            act.wait_ge(S["d_tr"], g * 16 + (q + 1))
                            act.wait_ge(S["d_used"], g * 16 + (q + 1))
                            s.activation(pt_sb[:, q % 2, :], ps_pt[:, q % 2, :], ACT.Copy).then_inc(S["d_ev"], 1)

                    G = n * H
                    add_source(G, 0, 0)
                    with act.Fori(0, H // 2 - 1) as hp:
                        for b in range(2):
                            head(G + hp * 2 + b, hp * 2 + b, b, False)
                    head(G + 6, 6, 0, False)
                    head(G + 7, 7, 1, True)
                    act.wait_ge(S["d_fin"], n * H + H)
                    act.dma_start(out[bass.ts(t, P), :], dout[:, :]).then_inc(S["d_out"], 16)
                    act.wait_ge(S["d_out"], n * 16 + 16)
                    act.sem_inc(S["d_free"], 1)
                    act.reg_add(done, done, 1)

        @block.tensor
        def _(pe):
            m = nc.tensor
            pe.wait_ge(S["ident_set"], 1)
            pe.wait_ge(S["w_in"], 32)
            pe.wait_ge(S["blk_in"], 16 * 16)
            for c in range(2):
                if c:
                    pe.wait_ge(S["wt_copied"], c)
                for q in range(2):
                    m.transpose(ps_w[:, q * P:(q + 1) * P], w_sb[:, q, c * P:(c + 1) * P], ident[:, :])
                    m.transpose(ps_w[:, HD + q * P:HD + (q + 1) * P], wr_sb[:, q, c * P:(c + 1) * P], ident[:, :])
                for q in range(2):
                    last = m.matmul(ps_w2[:, 0:16], w_sb[:, q, c * P:(c + 1) * P], a_blk[:, q, :],
                                    start=(q == 0), stop=(q == 1))
                last.then_inc(S["wt_done"], 1)
            pe.wait_ge(S["wt_copied"], 2)
            pe.wait_ge(S["small_in"], 48)

            def turn(u, q):
                pe.wait_ge(S["hn_done"], u + 1)
                for b in range(2):
                    for c in range(2):
                        last = m.transpose(ps_hnT[:, q % 2, b, c * P:(c + 1) * P],
                                           hn[:, q % 2, b, c * P:(c + 1) * P], ident[:, :])
                last.then_inc(S["hnT_ps"], 1)

            def maps(u, q):
                pe.wait_ge(S["hnT_done"], u + 1)
                if not isinstance(u, int) or u >= 2:
                    pe.wait_ge(S["dst_copied"], u - 1)
                    pe.wait_ge(S["res_done"], u - 1)
                q = q % 2
                for b in range(2):
                    for c in range(2):
                        rows = hnT[:, q, b, c * P:(c + 1) * P]
                        m.matmul(ps_hd[:, q, b, :], rows, w_all[:, c, 0:272], start=(c == 0), stop=(c == 1))
                    for c in range(2):
                        rows = hnT[:, q, b, c * P:(c + 1) * P]
                        m.matmul(ps_dst[0:H, q, b, :], w_all[:, c, HD:ROW], rows, start=(c == 0), stop=(c == 1))
                    for c in range(2):
                        rows = hnT[:, q, b, c * P:(c + 1) * P]
                        m.matmul(ps_res[:, q, b, :], rows, w_all[:, c, 272:528], start=(c == 0), stop=False)
                    last = m.matmul(ps_res[:, q, b, :], ones[0:1, :], brow[:, :], start=False, stop=True)
                last.then_inc(S["proj_done"], 1)

            turn(0, 0)
            for u in range(1, 4):
                turn(u, u)
                maps(u - 1, u - 1)
            with pe.Fori(1, UNITS // 4) as i:
                for q in range(4):
                    turn(4 * i + q, q)
                    maps(4 * i + (q - 1), (q - 1) % 4)
            maps(UNITS - 1, 3)

            for ph, (t0, t1, K, NS) in enumerate(PHASES):
                with pe.Fori(0, (t1 - t0) // 2) as i:
                    for b in range(2):
                        c = 2 * i + (b + t0 - FIRST)
                        g0 = 0 if K > GSLOTS // 2 else b * (GSLOTS // 2)
                        pe.wait_ge(S[f"res_in{b}"], i * 16 + 16 * ((t0 - FIRST) // 2 + 1))
                        m.matmul(ps_sum[:, b, :], ident[:, :], res_sb[:, b, :], start=True, stop=False)
                        for k in range(K):
                            if k % (K // 2) == 0:
                                pe.wait_ge(S["weighted"], c * 2 + (k // (K // 2) + 1))
                            last = m.matmul(ps_sum[:, b, :], ident[:, :], gath[:, g0 + k, 0:HD],
                                            start=False, stop=(k == K - 1))
                        last.then_inc(S["tile_sum"], 1)

            pe.wait_ge(S["flag_b"], TILES - FIRST)
            m.transpose(ps_flag[0:TILES, 0:P], flags[:, :], ident[:, :]).then_inc(S["fl_t"], 1)
            pe.wait_ge(S["fl_max"], 1)
            m.matmul(ps_flag_row[0:1, 0:TILES], flagT[:, :], ident[0:TILES, 0:TILES], start=True, stop=True
                     ).then_inc(S["fl_row"], 1)

            pe.sem_inc(S["d_pv"], 2)
            pe.sem_inc(S["d_used"], 2)
            done = pe.alloc_register("dense_pe")
            pe.reg_mov(done, 0)
            pe.wait_ge(S["fl_ready"], 1)
            with pe.Fori(0, TILES) as t:
                flag = pe.value_load(flag_row[0:1, bass.ds(t, 1)], min_val=0, max_val=1)
                with pe.If(flag > 0):
                    n = pe.snap(done)
                    with pe.Fori(0, H // 2) as hp:
                        for b in range(2):
                            g = n * H + hp * 2 + b
                            pe.wait_ge(S["d_exp"], g + 1)
                            pe.wait_ge(S["d_h"], g * 16 + 16)
                            hv = h_sb[:, :].rearrange("p (c d) -> p c d", d=D)

                            def weighted(q):
                                pe.wait_ge(S["d_ev"], g * 16 + (q + 1))
                                for r in range(4):
                                    last = m.matmul(ps_out[:, b, :], pt_sb[:, q % 2, r * P:(r + 1) * P],
                                                    hv[:, 4 * q + r, :], start=(q == 0 and r == 0),
                                                    stop=(q == 15 and r == 3))
                                return last.then_inc(S["d_used"], 1)

                            for q in range(16):
                                for r in range(4):
                                    last = m.transpose(ps_pt[:, q % 2, r * P:(r + 1) * P],
                                                       u_sb[b][:, (4 * q + r) * P:(4 * q + r + 1) * P], ident[:, :])
                                last.then_inc(S["d_tr"], 1)
                                if q:
                                    weighted(q - 1)
                            weighted(15)
                            pe.wait_ge(S["d_used"], (g + 1) * 16 + 2)
                            pe.sem_inc(S["d_pv"], 1)
                    pe.reg_add(done, done, 1)


_INS = ["x", "adj", "L0_gnn_W", "L0_gnn_We", "L0_gnn_be", "L0_gnn_a_src", "L0_gnn_a_dst", "L0_gnn_Wr", "L0_gnn_br"]
_OUTS = [((N, HD), "float32")]


def kernel(**inputs):
    import numpy as _np
    import concourse.bacc as _bacc
    from concourse import mybir as _mybir
    from concourse.bass_utils import run_bass_kernel_spmd as _run

    nc = _bacc.Bacc("TRN2", target_bir_lowering=False, num_devices=1)
    arrays, args = {}, []
    for name in _INS:
        a = _np.ascontiguousarray(inputs[name])
        arrays[f"in_{name}_dram"] = a
        args.append(nc.dram_tensor(f"in_{name}_dram", a.shape, _mybir.dt.from_np(a.dtype), kind="ExternalInput").ap())
    for i, (shape, dtype) in enumerate(_OUTS):
        dt = _mybir.dt.from_np(_np.dtype(dtype))
        args.append(nc.dram_tensor(f"out_{i}_dram", shape, dt, kind="ExternalOutput").ap())
    gat_kernel(nc, *args)
    r = _run(nc, [arrays], core_ids=[0])
    got = tuple(r.results[0][f"out_{i}_dram"] for i in range(len(_OUTS)))
    return got[0]
```

```python
from contextlib import ExitStack

import numpy as np
import concourse.bass as bass
from concourse import mybir

ALU = mybir.AluOpType
ACT = mybir.ActivationFunctionType
F32 = mybir.dt.float32
U32 = mybir.dt.uint32
I32 = mybir.dt.int32
AX_X = mybir.AxisListType.X

P = 128
N = 8192
IN = 256
H = 8
D = 32
HD = H * D
TILES = N // P
UNITS = TILES // 2
ROW = HD + H
ALPHA = 0.2
EPS = 1e-5
NEG = -1e30
PAD = 64
JBITS = 17
LOW = (1 << JBITS) - 1
GSLOTS = 94

FIRST = 1
PHASES = [(1, 2, 75, 45, 2.2), (2, 3, 61, 30, 1.8), (3, 4, 58, 22, 1.8), (4, 5, 50, 22, 1.8), (5, 6, 44, 22, 1.8),
          (6, 7, 42, 22, 1.8), (7, 8, 40, 22, 1.8), (8, 14, 36, 18, 1.6), (14, 20, 29, 14, 1.8),
          (20, 32, 25, 14, 1.8), (32, 54, 23, 9, 1.8), (54, 60, 22, 9, 1.8), (60, 64, 18, 9, 1.8)]
KMAX = 8 * (max(p[2] for p in PHASES) // 8 + 1)
VMAX = 8 * max(p[3] for p in PHASES)
DVE_PRE_END = 20
GROUP = 8
HALF = N // 2


class Phase:

    def __init__(self, spec, landed):
        self.t0, self.t1, self.K, self.segs, self.power = spec
        self.n = self.t1 - self.t0
        self.c0 = self.t0 - FIRST
        self.rounds = self.K // 8 + 1
        self.act_slots = 10 if self.K < 20 or self.K > 38 else 14 if self.K < 32 else 16
        self.dve_pre = self.t0 < DVE_PRE_END
        self.parts = 2 if self.K < 30 else 3 if self.K < 40 else 8
        self.landed = landed
        self.loop = self.n > 1

    def dve_parts(self):
        n = self.K - self.act_slots
        cuts = [n * i // self.parts for i in range(self.parts + 1)]
        return list(zip(cuts[:-1], cuts[1:]))

    def slots(self, b, lo, hi):
        if self.loop:
            return [(lo, self.half[b] + lo, hi - lo)]
        at, n = (self.start + lo) % GSLOTS, hi - lo
        first = min(n, GSLOTS - at)
        return [(lo, at, first)] + ([(lo + first, 0, n - first)] if n > first else [])

    def slot(self, b, k):
        return self.slots(b, k, k + 1)[0][1]


def plan():
    landed, phases, at, owner, half = [0, 0], [], 0, [None] * GSLOTS, None
    part_sums = 0
    for spec in PHASES:
        ph = Phase(spec, list(landed))
        assert ph.n == 1 or ph.n >= 4 and ph.n % 2 == 0
        ph.parts_before = sum(q.n * q.parts for q in phases)
        ph.act_before = sum(q.n * q.act_slots for q in phases)
        if ph.loop:
            if half is None:
                first = ph.c0 % 2
                half = [0, GSLOTS // 2] if first == 0 else [GSLOTS // 2, 0]
                for c in (ph.c0, ph.c0 + 1):
                    assert all(o is None or o[2] < c for o in owner[half[c % 2]:half[c % 2] + GSLOTS // 2 - (c == ph.c0)])
            assert ph.K <= GSLOTS // 2
            ph.half = half
        else:
            assert half is None
            ph.start = at
            ph.free_at = [owner[ph.slot(0, k)] for k in range(ph.K)]
            for n, (lo, hi) in enumerate(ph.dve_parts()):
                for k in range(lo, hi):
                    owner[ph.slot(0, k)] = ("part_sum", part_sums + n + 1, ph.c0 + 1)
            for k in range(ph.K - ph.act_slots, ph.K):
                owner[ph.slot(0, k)] = ("tile_sum", ph.c0 + 1, ph.c0 + 1)
            part_sums += ph.parts
            at = (at + ph.K) % GSLOTS
        for c in range(ph.c0, ph.c0 + ph.n):
            landed[c % 2] += 16 * ph.K
        phases.append(ph)
    return phases


def segments(n, power):
    bounds = [0]
    for s in range(1, n + 1):
        bounds.append(max(bounds[-1] + 8, int(round(N * (s / n) ** power))))
    return bounds


def gat_kernel(nc, x, adj, W, We, be, a_src, a_dst, Wr, br, out):
    table = nc.dram_tensor("table", (N + PAD, ROW), F32, kind="Internal").ap()
    resid = nc.dram_tensor("resid", (N, HD), F32, kind="Internal").ap()
    dst_rows = nc.dram_tensor("dst_rows", (H, N), F32, kind="Internal").ap()

    with ExitStack() as ctx:
        phases = plan()

        def sb(name, shape, dt=F32):
            return ctx.enter_context(nc.sbuf_tensor(name, shape, dt))

        def sem(name):
            return ctx.enter_context(nc.semaphore(name))

        banks = ctx.enter_context(nc.psum_tensor("banks", [P, 8, 512], F32))
        ps_hnT = banks[:, 0:2, :].rearrange("p u (b n) -> p u b n", b=2)
        ps_hd = banks[:, 2:6, 0:ROW + H].rearrange("p (u b) n -> p u b n", u=2)
        ps_dst = banks[:, 2:6, 384:512].rearrange("p (u b) n -> p u b n", u=2)
        ps_res = banks[:, 6:8, :].rearrange("p u (b n) -> p u b n", b=2)
        ps_w, ps_w2 = banks[:, 6, :], banks[:, 7, :]
        ps_sum = banks[:, 0:2, 0:HD]
        ps_pt = [banks[:, q, :] for q in (2, 3, 6, 7)]
        ps_acc = banks[0:D, 4:6, 0:P]
        ps_out = banks[:, 4:6, 256:256 + D]
        ps_flag, ps_flag_row = banks[:, 6, :], banks[:, 7, :]

        ident = sb("ident", [P, P])
        ones = sb("ones", [P, P])
        w_all = sb("w_all", [P, 2, 528])
        eps = sb("eps", [P, 1])
        br_all = sb("br_all", [P, HD])
        be_all = sb("be_all", [P, H])
        we_all = sb("we_all", [P, H])
        seg_base = {(n, w): sb(f"seg_base{n}", [P, n * 8]) for n, w in sorted({(ph.segs, ph.power) for ph in phases})}
        s_all = sb("s_all", [P, TILES, H])
        flags = sb("flags", [P, TILES])
        flagT = sb("flagT", [TILES, 1])
        flag_row = sb("flag_row", [1, TILES], I32)
        group_row = sb("group_row", [1, TILES // GROUP], I32)

        adj_sb = sb("adj_sb", [P, 2, N])
        gath = sb("gath", [P, GSLOTS, ROW])
        work = sb("work", [P, max(5 * VMAX + 4 * KMAX, 2 * TILES * D)])
        val8, idx8, jpad, key_lo, key_hi = (work[:, i * VMAX:(i + 1) * VMAX] for i in range(5))
        idx8, jpad, key_lo, key_hi = (w.bitcast(U32) for w in (idx8, jpad, key_lo, key_hi))
        slot_lo, slot_hi, jcol, far = (work[:, 5 * VMAX + i * KMAX:5 * VMAX + (i + 1) * KMAX] for i in range(4))
        slot_lo, slot_hi, jcol = (w.bitcast(U32) for w in (slot_lo, slot_hi, jcol))
        offs = sb("offs", [P, 2, KMAX], U32)
        aval = sb("aval", [P, 2, KMAX], U32)
        ahi = sb("ahi", [P, KMAX], U32)
        off_mask = sb("off_mask", [P, 2, KMAX])
        pre = sb("pre", [P, 2, KMAX * H])
        prob = sb("prob", [P, KMAX * H])
        flag8 = sb("flag8", [P, 1])
        rmax = sb("rmax", [P, H])
        rsum = sb("rsum", [P, H])
        rinv = sb("rinv", [P, H])
        res_sb = sb("res_sb", [P, 2, HD])
        out_sb = sb("out_sb", [P, 2, HD])

        gflat = gath[:, :, :].rearrange("p k r -> p (k r)")
        at = [0]

        def part(width):
            at[0] += width
            return gflat[:, at[0] - width:at[0]]

        w_sb = part(2 * IN).rearrange("p (q n) -> p q n", q=2)
        wr_sb = part(2 * IN).rearrange("p (q n) -> p q n", q=2)
        a_blk = part(32).rearrange("p (q n) -> p q n", q=2)
        x_sb = part(4 * 2 * IN).rearrange("p (u b n) -> p u b n", u=4, b=2)
        hn = part(2 * 2 * IN).rearrange("p (u b n) -> p u b n", u=2, b=2)
        hnT = part(2 * 2 * IN).rearrange("p (u b n) -> p u b n", u=2, b=2)
        hd_sb = part(2 * 2 * (ROW + H)).rearrange("p (u b n) -> p u b n", u=2, b=2)
        rt_sb = part(2 * 2 * HD).rearrange("p (u b n) -> p u b n", u=2, b=2)
        dst_sb = part(2 * 2 * P).rearrange("p (u b n) -> p u b n", u=2, b=2)
        stat = part(4 * 12).rearrange("p (u b n) -> p u b n", u=4, b=2)
        mv = part(4 * 4).rearrange("p (u b n) -> p u b n", u=4, b=2)
        rstd = part(4 * 2).rearrange("p (u b) -> p u b", u=4)
        sdev = part(4 * 2).rearrange("p (u b) -> p u b", u=4)
        assert at[0] <= GSLOTS * ROW
        bias_m = gflat[:, 0:N]
        dst_bc = gflat[:, N:2 * N]
        u_sb = [adj_sb[:, 1, :], gflat[:, 2 * N:3 * N]]
        a_t = adj_sb[:, 0, :]
        pt_sb = [pre[:, 0, 0:512], pre[:, 1, 0:512], w_all[:, 0, 0:512], w_all[:, 1, 0:512]]
        h_sb = [work[:, 0:TILES * D], work[:, TILES * D:2 * TILES * D]]
        ot_sb = sb("ot_sb", [D, 2, P])
        umax = sb("umax", [P, 2])
        ushift = sb("ushift", [P, 2])
        uleak = sb("uleak", [P, 2])
        nmax = sb("nmax", [P, 2])
        uden2 = sb("uden2", [P, 2, 2])
        uden = sb("uden", [P, 2])
        urec = sb("urec", [P, 2])
        dres = prob[:, 0:HD]
        dout = prob[:, HD:2 * HD]

        S = {n: sem(n) for n in (
            "ones_set", "held", "ident_set", "blk_zero", "blk_in", "w_in", "small_in", "wt_done", "wt_copied",
            "x_in0", "x_in1", "x_in2", "x_in3", "x_free", "bn_done", "mv_done", "sd_done", "eps_set", "rstd_done", "hn_done", "hnT_ps", "hnT_done",
            "proj_done", "hd_copied", "dst_copied", "s_done", "res_done", "br_added",
            "hd_out0", "hd_out1", "res_out0", "res_out1", "dst_out0", "dst_out1", "gath_zero", "pad_out", "base_set",
            "adj_in0", "adj_in1", "maxed", "scanned", "jadd", "jshift", "keyed", "masked_keys", "sorted_",
            "dec1", "dec2", "decoded", "az1", "az2", "pre_done", "flag_a", "flag_b",
            "gath_in0", "gath_in1", "z1", "z2", "z3", "z_ready", "exped", "summed_p", "recip", "normed",
            "weighted", "part_sum", "tile_sum", "out_copied", "out_st0", "out_st1", "res_in0", "res_in1",
            "fl_t", "fl_max", "fl_row", "fl_ready", "gr_ready", "act_weighted", "flag_init",
            "d_adj", "d_free", "d_mask", "d_ot", "d_oT", "d_dst0", "d_dst1", "d_w", "d_h0", "d_h1", "d_acc", "d_u1", "d_m1", "d_m2", "d_m", "d_leak", "d_own", "d_src", "d_exp",
            "d_tr", "d_ev", "d_used", "d_pv", "d_sum", "d_rec", "d_fin", "d_res", "d_out")}

        def hold(eng, semaphore, value):
            eng.wait_ge(semaphore, value)
            eng.sem_inc(S["held"], 1)

        def flagged_tiles(eng, body):
            with eng.Fori(0, TILES // GROUP) as gr:
                some = eng.value_load(group_row[0:1, bass.ds(gr, 1)], min_val=0, max_val=1)
                with eng.If(some > 0):
                    with eng.Fori(0, GROUP) as r:
                        t = gr * GROUP + r
                        flag = eng.value_load(flag_row[0:1, bass.ds(t, 1)], min_val=0, max_val=1)
                        with eng.If(flag > 0):
                            body(eng, t)

        def prepare(eng, e, ph, c, t, b):
            K = ph.K
            pv = pre[:, b, 0:K * H].rearrange("p (k h) -> p k h", h=H)
            e.tensor_tensor(pv, aval[:, b, 0:K].bitcast(F32).unsqueeze(2).to_broadcast([P, K, H]),
                            we_all[:, :].unsqueeze(1).to_broadcast([P, K, H]), ALU.mult).then_inc(S["az1"], 1)
            eng.wait_ge(S["az1"], c + 1)
            e.tensor_tensor(pv, pv, s_all[:, bass.ds(t, 1), :].to_broadcast([P, K, H]), ALU.add
                            ).then_inc(S["az2"], 1)
            eng.wait_ge(S["az2"], c + 1)
            e.tensor_tensor(pv, pv, off_mask[:, b, 0:K].unsqueeze(2).to_broadcast([P, K, H]), ALU.add
                            ).then_inc(S["pre_done"], 1)

        load_adj = lambda t: adj[bass.ts(t, P), :]
        by_unit = lambda a, u: a[bass.ts(u, 2 * P), :].rearrange("(b p) n -> p b n", p=P)
        block = ctx.enter_context(nc.Block())

        @block.sync
        def _(sp):
            sp.dma_start(w_sb, W.rearrange("(q p) n -> p q n", p=P)).then_inc(S["w_in"], 16)
            sp.dma_start(wr_sb, Wr.rearrange("(q p) n -> p q n", p=P)).then_inc(S["w_in"], 16)
            sp.dma_start(br_all[:, :], br.partition_broadcast(P)).then_inc(S["small_in"], 16)
            sp.dma_start(be_all[:, :], be.partition_broadcast(P)).then_inc(S["small_in"], 16)
            sp.dma_start(we_all[:, :], We.rearrange("h a -> (h a)").partition_broadcast(P)).then_inc(S["small_in"], 16)
            sp.wait_ge(S["blk_zero"], 1)
            for q in range(2):
                for r in range(4):
                    h = 4 * q + r
                    for o, a in ((0, a_dst), (H, a_src)):
                        sp.dma_start(a_blk[D * r:D * r + D, q, o + h:o + h + 1],
                                     a[h, :].rearrange("(d a) -> d a", a=1)).then_inc(S["blk_in"], 16)
            with sp.Fori(0, UNITS // 4) as i:
                for q in range(4):
                    u = 4 * i + q
                    sp.wait_ge(S["x_free"], u + 1)
                    sp.dma_start(x_sb[:, q, :, :], by_unit(x, u)).then_inc(S[f"x_in{q}"], 16)
            for ph in phases:
                def load(j):
                    t, c = j + ph.t0, j + ph.c0
                    b = (ph.c0 + (j if isinstance(j, int) else parity)) % 2
                    if not isinstance(c, int) or c >= 2:
                        sp.wait_ge(S["scanned"], c - 1)
                    sp.dma_start(adj_sb[:, b, :], load_adj(t)).then_inc(S[f"adj_in{b}"], 16)
                if not ph.loop:
                    load(0)
                else:
                    with sp.Fori(0, ph.n // 2) as i:
                        for parity in range(2):
                            load(2 * i + parity)
            sp.sem_inc(S["d_free"], 1)
            sp.sem_inc(S["d_u1"], 2)
            done = sp.alloc_register("dense_sp")
            sp.reg_mov(done, 0)
            sp.wait_ge(S["gr_ready"], 1)

            def dense_tile(sp, t):
                    n = sp.snap(done)
                    sp.wait_ge(S["d_free"], n + 1)
                    sp.dma_start(a_t, load_adj(t)).then_inc(S["d_adj"], 16)
                    sp.dma_start(dres[:, :], resid[bass.ts(t, P), :]).then_inc(S["d_res"], 16)
                    with sp.Fori(0, H // 2) as hp:
                        for b in range(2):
                            g = n * H + hp * 2 + b
                            h = hp * 2 + b
                            for r in range(2):
                                sp.wait_ge(S["d_u1"], g * 2 + (r + 1))
                                sp.dma_start(dst_bc[:, r * HALF:(r + 1) * HALF],
                                             dst_rows[bass.ds(h, 1), r * HALF:(r + 1) * HALF].partition_broadcast(P)[:, 0, :]
                                             ).then_inc(S[f"d_dst{r}"], 16)
                            sp.wait_ge(S["d_pv"], g + 1)
                            sp.dma_start(h_sb[b][:, :].rearrange("p (c d) -> p c d", d=D),
                                         table[PAD:, :].rearrange("(c p) r -> p c r", p=P)[:, :, bass.ts(h, D)]
                                         ).then_inc(S[f"d_h{b}"], 16)
                    sp.reg_add(done, done, 1)

            flagged_tiles(sp, dense_tile)

        @block.gpsimd
        def _(pool):
            pool.memset(ones[:, :], 1.0).then_inc(S["ones_set"], 1)
            pool.memset(eps[:, :], EPS).then_inc(S["eps_set"], 1)
            pool.memset(a_blk, 0.0).then_inc(S["blk_zero"], 1)
            pool.memset(flags[:, :], 1.0).then_inc(S["flag_init"], 1)
            for (n, power), base in seg_base.items():
                bounds = segments(n, power)
                for s in range(n):
                    last = pool.memset(base[:, 8 * s:8 * s + 8], float(bounds[s] + PAD))
            last.then_inc(S["base_set"], 1)
            pool.wait_ge(S["ones_set"], 1)
            pool.affine_select(out=ident[:, :], in_=ones[:, :], compare_op=ALU.is_equal, fill=0.0,
                               base=0, pattern=[[-1, P]], channel_multiplier=1).then_inc(S["ident_set"], 1)
            pool.wait_ge(S["small_in"], 48)
            with pool.Fori(0, UNITS // 2) as i:
                for q in range(2):
                    u = 2 * i + q
                    pool.wait_ge(S["hd_copied"], u + 1)
                    pool.dma_start(by_unit(table[PAD:, :], u), hd_sb[:, q, :, 0:ROW]).then_inc(S[f"hd_out{q}"], 16)
                    pool.wait_ge(S["dst_copied"], u + 1)
                    pool.dma_start(dst_rows[:, bass.ts(u, 2 * P)].rearrange("h (b p) -> h b p", b=2),
                                   dst_sb[0:H, q, :, :]).then_inc(S[f"dst_out{q}"], 16)
                    pool.wait_ge(S["res_done"], u + 1)
                    nc.gpsimd.tensor_tensor(rt_sb[:, q, :, :], rt_sb[:, q, :, :],
                                            br_all[:, :].unsqueeze(1).to_broadcast([P, 2, HD]), ALU.add
                                            ).then_inc(S["br_added"], 1)
                    pool.wait_ge(S["br_added"], u + 1)
                    pool.dma_start(by_unit(resid, u), rt_sb[:, q, :, :]).then_inc(S[f"res_out{q}"], 16)
            for b in range(2):
                for q in ("hd_out", "dst_out", "res_out"):
                    pool.wait_ge(S[f"{q}{b}"], 16 * (UNITS // 2))
            pool.memset(gflat, 0.0).then_inc(S["gath_zero"], 1)
            pool.wait_ge(S["gath_zero"], 1)
            pool.dma_start(table[0:PAD, :], gath[0:PAD, 0, :]).then_inc(S["pad_out"], 16)
            pool.wait_ge(S["pad_out"], 16)

            def gather(ph, j, b):
                c, t, K = j + ph.c0, j + ph.t0, ph.K
                pool.wait_ge(S["decoded"], c + 1)
                if not ph.dve_pre:
                    prepare(pool, nc.gpsimd, ph, c, t, b)
                waited = {"part_sum": 0, "tile_sum": 0}
                if ph.loop:
                    hold(pool, S["tile_sum"], c - 1)
                for k in range(K):
                    if not ph.loop and ph.free_at[k]:
                        summed, value, _ = ph.free_at[k]
                        if value > waited[summed]:
                            waited[summed] = value
                            pool.wait_ge(S[summed], value)
                    pool.indirect_dma_start(
                        gath[:, ph.slot(b, k), :], None, table[:, :],
                        bass.IndirectOffsetOnAxis(ap=offs[:, b, k:k + 1], axis=0),
                        bounds_check=N + PAD - 1, oob_is_err=False).then_inc(S[f"gath_in{b}"], 16)

            for ph in phases:
                if not ph.loop:
                    gather(ph, 0, ph.c0 % 2)
                else:
                    with pool.Fori(0, ph.n // 2) as i:
                        for q in range(2):
                            gather(ph, 2 * i + q, (ph.c0 + q) % 2)

            done = pool.alloc_register("dense_pool")
            pool.reg_mov(done, 0)
            pool.wait_ge(S["gr_ready"], 1)

            def dense_tile(pool, t):
                    n = pool.snap(done)
                    hold(pool, S["d_mask"], n + 1)
                    with pool.Fori(0, H) as h:
                        for r in range(2):
                            pool.wait_ge(S[f"d_dst{r}"], n * (16 * H) + (h * 16 + 16))
                            half = slice(r * HALF, (r + 1) * HALF)
                            nc.gpsimd.tensor_tensor(dst_bc[:, half], dst_bc[:, half], bias_m[:, half], ALU.add
                                                    ).then_inc(S["d_w"], 1)
                    pool.reg_add(done, done, 1)

            flagged_tiles(pool, dense_tile)

        @block.vector
        def _(dve):
            v = nc.vector
            for c in range(2):
                dve.wait_ge(S["wt_done"], c + 1)
                v.tensor_copy(w_all[:, c, 0:HD], ps_w[:, 0:HD])
                v.tensor_copy(w_all[:, c, 272:528], ps_w[:, HD:2 * HD])
                v.tensor_copy(w_all[:, c, HD:HD + 16], ps_w2[:, 0:16]).then_inc(S["wt_copied"], 1)
            dve.sem_inc(S["x_free"], 4)
            dve.wait_ge(S["small_in"], 48)

            def normalize(u, q):
                i = u // 4 if isinstance(u, int) else u >> 2
                dve.wait_ge(S[f"x_in{q}"], 16 * i + 16)
                for b in range(2):
                    last = v.bn_stats(stat[:, q, b, :], x_sb[:, q, b, :])
                last.then_inc(S["bn_done"], 1)
                hold(dve, S["bn_done"], u + 1)
                for b in range(2):
                    last = v.bn_aggr(mv[:, q, b, :], stat[:, q, b, :])
                last.then_inc(S["mv_done"], 1)
                dve.wait_ge(S["sd_done"], u + 1)
                v.reciprocal(rstd[:, q, :], sdev[:, q, :]).then_inc(S["rstd_done"], 1)
                dve.wait_ge(S["rstd_done"], u + 1)
                if not isinstance(u, int) or u >= 2:
                    dve.wait_ge(S["hnT_ps"], u - 1)
                for b in range(2):
                    last = v.tensor_scalar(hn[:, q % 2, b, :], x_sb[:, q, b, :], mv[:, q, b, 0:1],
                                           rstd[:, q, b:b + 1], ALU.subtract, ALU.mult)
                last.then_inc(S["hn_done"], 1)

            def add_biases(u, q):
                dve.wait_ge(S["hd_copied"], u + 1)
                v.tensor_tensor(s_all[:, bass.ts(u, 2), :], hd_sb[:, q % 2, :, ROW:ROW + H],
                                be_all[:, :].unsqueeze(1).to_broadcast([P, 2, H]), ALU.add).then_inc(S["s_done"], 1)
                if not isinstance(u, int):
                    dve.wait_ge(S[f"res_out{q % 2}"], (u >> 1) * 16)
                elif u >= 2:
                    dve.wait_ge(S[f"res_out{q % 2}"], u // 2 * 16)
                v.tensor_tensor(rt_sb[:, q % 2, :, :], ps_res[:, q % 2, :, :], x_sb[:, q, :, :], ALU.add
                                ).then_inc(S["res_done"], 1)
                hold(dve, S["res_done"], u + 1)
                dve.sem_inc(S["x_free"], 1)

            for u in range(4):
                normalize(u, u % 4)
                if u >= 2:
                    add_biases(u - 2, (u - 2) % 4)
            with dve.Fori(1, UNITS // 4) as i:
                for q in range(4):
                    normalize(4 * i + q, q)
                    add_biases(4 * i + (q - 2), (q - 2) % 4)
            for u in range(UNITS - 2, UNITS):
                add_biases(u, u % 4)

            dve.wait_ge(S["base_set"], 1)
            dve.wait_ge(S["flag_init"], 1)
            dve.wait_ge(S["s_done"], UNITS)
            sorted_before, r = [], 0
            for ph in phases:
                sorted_before.append(r)
                r += ph.n * 2 * ph.rounds

            def halved(c):
                return c // 2 if isinstance(c, int) else c >> 1

            def find(p, j, b):
                ph = phases[p]
                c = j + ph.c0
                VN = 8 * ph.segs
                bounds = segments(ph.segs, ph.power)
                hold(dve, S[f"adj_in{b}"], halved(c) * 16 + 16)
                a = adj_sb[:, b, :]
                for s in range(ph.segs):
                    last = v.max(val8[:, 8 * s:8 * s + 8], a[:, bounds[s]:bounds[s + 1]])
                last.then_inc(S["maxed"], 1)
                hold(dve, S["maxed"], c + 1)
                for s in range(ph.segs):
                    last = v.max_index(idx8[:, 8 * s:8 * s + 8], val8[:, 8 * s:8 * s + 8],
                                       a[:, bounds[s]:bounds[s + 1]])
                last.then_inc(S["scanned"], 1)
                v.tensor_reduce(flag8[:, :], val8[:, 0:VN].rearrange("p (s e) -> p s e", e=8)[:, :, 7],
                                AX_X, ALU.max).then_inc(S["flag_a"], 1)
                dve.wait_ge(S["scanned"], c + 1)
                v.tensor_tensor(jpad[:, 0:VN], idx8[:, 0:VN], seg_base[ph.segs, ph.power][:, :], ALU.add).then_inc(S["jadd"], 1)
                dve.wait_ge(S["jadd"], c + 1)
                v.scalar_tensor_tensor(out=jpad[:, 0:VN], in0=val8[:, 0:VN], scalar=0.0, in1=jpad[:, 0:VN],
                                       op0=ALU.is_gt, op1=ALU.mult).then_inc(S["masked_keys"], 1)
                dve.wait_ge(S["masked_keys"], c + 1)
                v.tensor_scalar(idx8[:, 0:VN], jpad[:, 0:VN], JBITS, None, ALU.logical_shift_left
                                ).then_inc(S["jshift"], 1)
                dve.wait_ge(S["jshift"], c + 1)
                vb = val8[:, 0:VN].bitcast(U32)
                v.scalar_tensor_tensor(out=key_lo[:, 0:VN], in0=vb, scalar=LOW, in1=idx8[:, 0:VN],
                                       op0=ALU.bitwise_and, op1=ALU.bitwise_or)
                v.scalar_tensor_tensor(out=key_hi[:, 0:VN], in0=vb, scalar=JBITS, in1=idx8[:, 0:VN],
                                       op0=ALU.logical_shift_right, op1=ALU.bitwise_or).then_inc(S["keyed"], 1)
                hold(dve, S["keyed"], c + 1)

            def sort_step(p, j, m):
                ph = phases[p]
                K, R, VN, q = ph.K, ph.rounds, 8 * ph.segs, m // 2
                kl, kh = key_lo[:, 0:VN].bitcast(F32), key_hi[:, 0:VN].bitcast(F32)
                sl, sh = slot_lo[:, 8 * q:8 * q + 8].bitcast(F32), slot_hi[:, 8 * q:8 * q + 8].bitcast(F32)
                if m:
                    hold(dve, S["sorted_"], j * (2 * R) + (sorted_before[p] + m))
                if m % 2 == 0:
                    v.max(sl, kl)
                    v.max(sh, kh).then_inc(S["sorted_"], 1)
                elif q < R - 1:
                    v.match_replace(kl, sl, kl, 0.0)
                    v.match_replace(kh, sh, kh, 0.0).then_inc(S["sorted_"], 1)
                else:
                    v.tensor_scalar(jcol[:, 0:K], slot_lo[:, 0:K], JBITS, None, ALU.logical_shift_right
                                    ).then_inc(S["sorted_"], 1)

            def decode(p, j, b):
                ph = phases[p]
                c, t, K = j + ph.c0, j + ph.t0, ph.K
                hold(dve, S["sorted_"], j * (2 * ph.rounds) + (sorted_before[p] + 2 * ph.rounds))
                v.tensor_scalar(far[:, 0:K], jcol[:, 0:K], 1.0, float(2 * N), ALU.is_lt, ALU.mult)
                v.tensor_scalar(off_mask[:, b, 0:K], jcol[:, 0:K], 1.0, NEG, ALU.is_lt, ALU.mult
                                ).then_inc(S["dec1"], 1)
                v.tensor_scalar(ahi[:, 0:K], slot_hi[:, 0:K], JBITS, 0x7FFFFFFF, ALU.logical_shift_left,
                                ALU.bitwise_and).then_inc(S["dec2"], 1)
                dve.wait_ge(S["dec1"], c + 1)
                v.tensor_tensor(offs[:, b, 0:K], jcol[:, 0:K], far[:, 0:K], ALU.add)
                dve.wait_ge(S["dec2"], c + 1)
                v.scalar_tensor_tensor(out=aval[:, b, 0:K], in0=slot_lo[:, 0:K], scalar=LOW, in1=ahi[:, 0:K],
                                       op0=ALU.bitwise_and, op1=ALU.bitwise_or).then_inc(S["decoded"], 1)
                dve.wait_ge(S["flag_a"], c + 1)
                v.tensor_tensor(flags[:, bass.ds(t, 1)], flag8[:, :], slot_lo[:, K:K + 1].bitcast(F32), ALU.max
                                ).then_inc(S["flag_b"], 1)
                if ph.dve_pre:
                    dve.wait_ge(S["decoded"], c + 1)
                    prepare(dve, v, ph, c, t, b)

            def softmax_step(p, j, b, m):
                ph = phases[p]
                c, K = j + ph.c0, ph.K
                z, pr = pre[:, b, 0:K * H], prob[:, 0:K * H]
                zv, prv = (w.rearrange("p (k h) -> p k h", h=H) for w in (z, pr))
                zh, prh = (w.rearrange("p (k h) -> p h k", h=H) for w in (z, pr))
                if m == 0:
                    if isinstance(j, int):
                        turn = (j - (b - ph.c0) % 2) // 2
                    else:
                        turn = j >> 1
                    dve.wait_ge(S[f"gath_in{b}"], turn * (16 * K) + (ph.landed[b] + 16 * K))
                    dve.wait_ge(S["pre_done"], c + 1)
                    for k, at, n in ph.slots(b, 0, K):
                        last = v.tensor_tensor(zv[:, k:k + n, :], zv[:, k:k + n, :], gath[:, at:at + n, HD:ROW], ALU.add)
                    last.then_inc(S["z1"], 1)
                elif m == 1:
                    dve.wait_ge(S["z1"], c + 1)
                    v.scalar_tensor_tensor(out=z, in0=z, scalar=ALPHA, in1=z, op0=ALU.mult, op1=ALU.max
                                           ).then_inc(S["z2"], 1)
                elif m == 2:
                    dve.wait_ge(S["z2"], c + 1)
                    v.tensor_reduce(rmax[:, :], zh, AX_X, ALU.max).then_inc(S["z3"], 1)
                elif m == 3:
                    dve.wait_ge(S["z3"], c + 1)
                    v.tensor_tensor(zv, zv, rmax[:, :].unsqueeze(1).to_broadcast([P, K, H]), ALU.subtract
                                    ).then_inc(S["z_ready"], 1)
                elif m == 5:
                    dve.wait_ge(S["exped"], c + 1)
                    v.tensor_reduce(rsum[:, :], prh, AX_X, ALU.add).then_inc(S["summed_p"], 1)
                elif m == 6:
                    dve.wait_ge(S["summed_p"], c + 1)
                    v.reciprocal(rinv[:, :], rsum[:, :]).then_inc(S["recip"], 1)
                elif m == 7:
                    dve.wait_ge(S["recip"], c + 1)
                    v.tensor_tensor(prv, prv, rinv[:, :].unsqueeze(1).to_broadcast([P, K, H]), ALU.mult
                                    ).then_inc(S["normed"], 1)

            def weight(p, j, b):
                ph = phases[p]
                c = j + ph.c0
                dve.wait_ge(S["normed"], c + 1)
                for lo, hi in ph.dve_parts():
                    for k, at, n in ph.slots(b, lo, hi):
                        gv = gath[:, at:at + n, 0:HD].rearrange("p k (h d) -> p k h d", d=D)
                        pb = prob[:, k * H:(k + n) * H].rearrange("p (k h) -> p k h", h=H)
                        last = v.tensor_tensor(gv, gv, pb.unsqueeze(3).to_broadcast([P, n, H, D]), ALU.mult)
                    last.then_inc(S["weighted"], 1)

            par = lambda ph, q: (ph.c0 + q) % 2
            order = [(p, j) for p, ph in enumerate(phases) for j in range(ph.n)]

            def step(p, j, b, pn, jn):
                steps = 0 if pn is None else 2 * phases[pn].rounds
                if pn is not None:
                    find(pn, jn, b)
                for m in range(max(steps, 8)):
                    if m < steps:
                        sort_step(pn, jn, m)
                    softmax_step(p, j, b, m)
                weight(p, j, b)
                if pn is not None:
                    decode(pn, jn, b)

            for c in range(2):
                p, j = order[c]
                find(p, j, c)
                for m in range(2 * phases[p].rounds):
                    sort_step(p, j, m)
                decode(p, j, c)
            for p, ph in enumerate(phases):
                if ph.loop:
                    with dve.Fori(0, ph.n // 2 - 1) as i:
                        for q in range(2):
                            step(p, 2 * i + q, par(ph, q), p, 2 * i + (q + 2))
                for j in range(ph.n - 2 if ph.loop else 0, ph.n):
                    c = ph.c0 + j
                    step(p, j, c % 2, *(order[c + 2] if c + 2 < len(order) else (None, None)))

            dve.wait_ge(S["fl_t"], 1)
            v.tensor_reduce(flagT[:, :], ps_flag[0:TILES, 0:P], AX_X, ALU.max).then_inc(S["fl_max"], 1)
            dve.wait_ge(S["fl_row"], 1)
            v.tensor_scalar(flag_row[:, :], ps_flag_row[0:1, 0:TILES], 0.0, None, ALU.is_gt).then_inc(S["fl_ready"], 1)
            dve.wait_ge(S["fl_ready"], 1)
            v.tensor_reduce(group_row[:, :], flag_row[:, :].rearrange("p (g r) -> p g r", r=GROUP), AX_X, ALU.max
                            ).then_inc(S["gr_ready"], 1)

            done = dve.alloc_register("dense_dve")
            dve.reg_mov(done, 0)
            dve.wait_ge(S["gr_ready"], 1)

            def dense_tile(dve, t):
                    n = dve.snap(done)
                    dve.wait_ge(S["d_adj"], n * 16 + 16)
                    v.tensor_scalar(bias_m, a_t, 0.0, NEG, ALU.is_le, ALU.mult).then_inc(S["d_mask"], 1)
                    hold(dve, S["d_mask"], n + 1)

                    def scores(g, h, b):
                        u = [u_sb[b][:, r * HALF:(r + 1) * HALF] for r in range(2)]

                        def leak(r):
                            v.scalar_tensor_tensor(out=u[r], in0=u[r], scalar=ALPHA, in1=u[r],
                                                   op0=ALU.mult, op1=ALU.max).then_inc(S["d_leak"], 1)

                        hold(dve, S["d_pv"], g + 1)
                        v.tensor_scalar(u[0], a_t[:, 0:HALF], we_all[:, bass.ds(h, 1)],
                                        s_all[:, bass.ds(t, 1), bass.ds(h, 1)].rearrange("p a h -> p (a h)"),
                                        ALU.mult, ALU.add).then_inc(S["d_own"], 1)
                        for r in range(2):
                            hold(dve, S["d_src"] if r else S["d_own"], g + 1)
                            hold(dve, S["d_w"], g * 2 + (r + 1))
                            v.tensor_tensor_reduce(u[r], u[r], dst_bc[:, r * HALF:(r + 1) * HALF], 1.0, -3e38,
                                                   ALU.add, ALU.max, umax[:, r:r + 1]).then_inc(S["d_u1"], 1)
                        dve.wait_ge(S["d_u1"], g * 2 + 3)
                        leak(0)
                        dve.wait_ge(S["d_u1"], g * 2 + 4)
                        v.tensor_tensor(ushift[:, b:b + 1], umax[:, 0:1], umax[:, 1:2], ALU.max).then_inc(S["d_m1"], 1)
                        dve.wait_ge(S["d_m1"], g + 1)
                        v.scalar_tensor_tensor(out=uleak[:, b:b + 1], in0=ushift[:, b:b + 1], scalar=ALPHA,
                                               in1=ushift[:, b:b + 1], op0=ALU.mult, op1=ALU.max
                                               ).then_inc(S["d_m2"], 1)
                        dve.wait_ge(S["d_m2"], g + 1)
                        v.tensor_scalar(nmax[:, b:b + 1], uleak[:, b:b + 1], -1.0, None, ALU.mult
                                        ).then_inc(S["d_m"], 1)
                        leak(1)

                    def finish(g, h, b):
                        dve.wait_ge(S["d_exp"], g * 2 + 2)
                        v.tensor_tensor(uden[:, b:b + 1], uden2[:, b, 0:1], uden2[:, b, 1:2], ALU.add
                                        ).then_inc(S["d_sum"], 1)
                        dve.wait_ge(S["d_sum"], g + 1)
                        v.reciprocal(urec[:, b:b + 1], uden[:, b:b + 1]).then_inc(S["d_rec"], 1)
                        dve.wait_ge(S["d_rec"], g + 1)
                        dve.wait_ge(S["d_oT"], g + 1)
                        v.scalar_tensor_tensor(out=dout[:, bass.ts(h, D)], in0=ps_out[:, b, :],
                                               scalar=urec[:, b:b + 1], in1=dres[:, bass.ts(h, D)],
                                               op0=ALU.mult, op1=ALU.add).then_inc(S["d_fin"], 1)

                    hold(dve, S["d_res"], n * 16 + 16)
                    G = n * H
                    scores(G, 0, 0)
                    with dve.Fori(0, H // 2 - 1) as hp:
                        h = hp * 2
                        scores(G + h + 1, h + 1, 1)
                        finish(G + h, h, 0)
                        scores(G + h + 2, h + 2, 0)
                        finish(G + h + 1, h + 1, 1)
                    scores(G + 7, 7, 1)
                    finish(G + 6, 6, 0)
                    finish(G + 7, 7, 1)
                    dve.reg_add(done, done, 1)

            flagged_tiles(dve, dense_tile)

        @block.scalar
        def _(act):
            s = nc.scalar
            act.wait_ge(S["eps_set"], 1)
            def deviation(u, q):
                act.wait_ge(S["mv_done"], u + 1)
                s.activation(sdev[:, q, :], mv[:, q, :, 1], ACT.Sqrt, bias=eps[:, :]).then_inc(S["sd_done"], 1)

            def relu(u, q):
                act.wait_ge(S["hnT_ps"], u + 1)
                s.activation(hnT[:, q % 2, :, :], ps_hnT[:, q % 2, :, :], ACT.Relu).then_inc(S["hnT_done"], 1)

            def copies(u, q):
                act.wait_ge(S["proj_done"], u + 1)
                if not isinstance(u, int) or u >= 2:
                    half = u // 2 if isinstance(u, int) else u >> 1
                    act.wait_ge(S[f"hd_out{q % 2}"], half * 16)
                    act.wait_ge(S[f"dst_out{q % 2}"], half * 16)
                    act.wait_ge(S["s_done"], u - 1)
                s.activation(hd_sb[:, q % 2, :, :], ps_hd[:, q % 2, :, :], ACT.Copy).then_inc(S["hd_copied"], 1)
                s.activation(dst_sb[0:H, q % 2, :, :], ps_dst[0:H, q % 2, :, :], ACT.Copy).then_inc(S["dst_copied"], 1)

            deviation(0, 0)
            deviation(1, 1)
            relu(0, 0)
            deviation(2, 2)
            relu(1, 1)
            copies(0, 0)
            with act.Fori(0, UNITS // 4 - 1) as i:
                for q in range(4):
                    deviation(4 * i + (q + 3), (q + 3) % 4)
                    relu(4 * i + (q + 2), (q + 2) % 4)
                    copies(4 * i + (q + 1), (q + 1) % 4)
            deviation(UNITS - 1, 3)
            relu(UNITS - 2, 2)
            copies(UNITS - 3, 1)
            relu(UNITS - 1, 3)
            copies(UNITS - 2, 2)
            copies(UNITS - 1, 3)
            for b in range(2):
                act.wait_ge(S[f"res_out{b}"], 16 * (UNITS // 2))

            def load_res(t, b):
                act.dma_start(res_sb[:, b, :], resid[bass.ts(t, P), :]).then_inc(S[f"res_in{b}"], 16)

            def exps(p, j, b):
                ph = phases[p]
                c, K = j + ph.c0, ph.K
                act.wait_ge(S["z_ready"], c + 1)
                s.activation(prob[:, 0:K * H], pre[:, b, 0:K * H], ACT.Exp).then_inc(S["exped"], 1)
                act.wait_ge(S["normed"], c + 1)
                for k in range(K - ph.act_slots, K):
                    for h in range(H):
                        g = gath[:, ph.slot(b, k), h * D:(h + 1) * D]
                        last = s.activation(g, g, ACT.Copy, scale=prob[:, k * H + h:k * H + h + 1])
                    last.then_inc(S["act_weighted"], 1)

            def store(p, j, b):
                ph = phases[p]
                c, t = j + ph.c0, j + ph.t0
                act.wait_ge(S["tile_sum"], c + 1)
                if not isinstance(c, int):
                    act.wait_ge(S[f"out_st{b}"], (c >> 1) * 16)
                elif c >= 2:
                    act.wait_ge(S[f"out_st{b}"], c // 2 * 16)
                s.activation(out_sb[:, b, :], ps_sum[:, b, :], ACT.Copy).then_inc(S["out_copied"], 1)
                if not isinstance(t, int) or t + 2 < TILES:
                    load_res(t + 2, b)
                act.wait_ge(S["out_copied"], c + 1)
                act.dma_start(out[bass.ts(t, P), :], out_sb[:, b, :]).then_inc(S[f"out_st{b}"], 16)

            load_res(FIRST, 0)
            load_res(FIRST + 1, 1)
            par = lambda ph, q: (ph.c0 + q) % 2
            exps(0, 0, 0)
            for p, ph in enumerate(phases):
                if ph.loop:
                    with act.Fori(0, ph.n // 2 - 1) as i:
                        for q in range(2):
                            exps(p, 2 * i + (q + 1), par(ph, q + 1))
                            store(p, 2 * i + q, par(ph, q))
                    exps(p, ph.n - 1, par(ph, 1))
                    store(p, ph.n - 2, par(ph, 0))
                if p + 1 < len(phases):
                    exps(p + 1, 0, par(phases[p + 1], 0))
                store(p, ph.n - 1, par(ph, ph.n - 1))
            for b in range(2):
                act.wait_ge(S[f"out_st{b}"], 16 * ((TILES - FIRST + 1 - b) // 2))

            done = act.alloc_register("dense_act")
            act.reg_mov(done, 0)
            act.wait_ge(S["gr_ready"], 1)

            def dense_tile(act, t):
                    n = act.snap(done)

                    def edge_scores(g, h, b):
                        hold(act, S["d_pv"], g + 1)
                        half = slice(HALF, N)
                        s.activation(u_sb[b][:, half], a_t[:, half], ACT.Identity, scale=we_all[:, bass.ds(h, 1)],
                                     bias=s_all[:, bass.ds(t, 1), bass.ds(h, 1)].rearrange("p a h -> p (a h)")
                                     ).then_inc(S["d_src"], 1)

                    def exponentials(g, b, r):
                        act.wait_ge(S["d_leak"], g * 2 + (r + 1))
                        act.wait_ge(S["d_m"], g + 1)
                        u = u_sb[b][:, r * HALF:(r + 1) * HALF]
                        s.activation(u, u, ACT.Exp, bias=nmax[:, b:b + 1], accum_out=uden2[:, b, r:r + 1]
                                     ).then_inc(S["d_exp"], 1)

                    def sums_out(g, b):
                        act.wait_ge(S["d_acc"], g + 1)
                        s.activation(ot_sb[:, b, :], ps_acc[:, b, :], ACT.Copy).then_inc(S["d_ot"], 1)

                    def head(g, h, b, first=False, last=False):
                        exponentials(g, b, 0)
                        if not first:
                            sums_out(g - 1, 1 - b)
                        for q in range(16):
                            if q == 2 and not last:
                                edge_scores(g + 1, h + 1, 1 - b)
                            if q == 6:
                                exponentials(g, b, 1)
                            act.wait_ge(S["d_tr"], g * 16 + (q + 1))
                            act.wait_ge(S["d_used"], g * 16 + (q + 1))
                            s.activation(pt_sb[q % 4], ps_pt[q % 4], ACT.Copy).then_inc(S["d_ev"], 1)

                    G = n * H
                    act.wait_ge(S["d_adj"], n * 16 + 16)
                    edge_scores(G, 0, 0)
                    head(G, 0, 0, first=True)
                    with act.Fori(0, H // 2 - 1) as hp:
                        for h in (1, 2):
                            head(G + hp * 2 + h, hp * 2 + h, h % 2)
                    head(G + 7, 7, 1, last=True)
                    sums_out(G + 7, 1)
                    act.wait_ge(S["d_fin"], n * H + H)
                    act.dma_start(out[bass.ts(t, P), :], dout[:, :]).then_inc(S["d_out"], 16)
                    act.wait_ge(S["d_out"], n * 16 + 16)
                    act.sem_inc(S["d_free"], 1)
                    act.reg_add(done, done, 1)

            flagged_tiles(act, dense_tile)

        @block.tensor
        def _(pe):
            m = nc.tensor
            pe.wait_ge(S["ident_set"], 1)
            pe.wait_ge(S["w_in"], 32)
            pe.wait_ge(S["blk_in"], 16 * 16)
            for c in range(2):
                if c:
                    pe.wait_ge(S["wt_copied"], c)
                for q in range(2):
                    m.transpose(ps_w[:, q * P:(q + 1) * P], w_sb[:, q, c * P:(c + 1) * P], ident[:, :])
                    m.transpose(ps_w[:, HD + q * P:HD + (q + 1) * P], wr_sb[:, q, c * P:(c + 1) * P], ident[:, :])
                for q in range(2):
                    last = m.matmul(ps_w2[:, 0:16], w_sb[:, q, c * P:(c + 1) * P], a_blk[:, q, :],
                                    start=(q == 0), stop=(q == 1))
                last.then_inc(S["wt_done"], 1)
            pe.wait_ge(S["wt_copied"], 2)

            def turn(u, q):
                pe.wait_ge(S["hn_done"], u + 1)
                for b in range(2):
                    for c in range(2):
                        last = m.transpose(ps_hnT[:, q % 2, b, c * P:(c + 1) * P],
                                           hn[:, q % 2, b, c * P:(c + 1) * P], ident[:, :])
                last.then_inc(S["hnT_ps"], 1)

            def maps(u, q):
                pe.wait_ge(S["hnT_done"], u + 1)
                if not isinstance(u, int) or u >= 2:
                    pe.wait_ge(S["dst_copied"], u - 1)
                    pe.wait_ge(S["res_done"], u - 1)
                q = q % 2
                for b in range(2):
                    for c in range(2):
                        rows = hnT[:, q, b, c * P:(c + 1) * P]
                        m.matmul(ps_hd[:, q, b, :], rows, w_all[:, c, 0:272], start=(c == 0), stop=(c == 1))
                    for c in range(2):
                        rows = hnT[:, q, b, c * P:(c + 1) * P]
                        m.matmul(ps_dst[0:H, q, b, :], w_all[:, c, HD:ROW], rows, start=(c == 0), stop=(c == 1))
                    for c in range(2):
                        rows = hnT[:, q, b, c * P:(c + 1) * P]
                        last = m.matmul(ps_res[:, q, b, :], rows, w_all[:, c, 272:528], start=(c == 0), stop=(c == 1))
                last.then_inc(S["proj_done"], 1)

            turn(0, 0)
            for u in range(1, 4):
                turn(u, u)
                maps(u - 1, u - 1)
            with pe.Fori(1, UNITS // 4) as i:
                for q in range(4):
                    turn(4 * i + q, q)
                    maps(4 * i + (q - 1), (q - 1) % 4)
            maps(UNITS - 1, 3)

            def tile_sums(ph, j, b):
                c, K = j + ph.c0, ph.K
                pe.wait_ge(S[f"res_in{b}"], (c // 2 if isinstance(c, int) else c >> 1) * 16 + 16)
                if not isinstance(c, int) or c >= 2:
                    pe.wait_ge(S["out_copied"], c - 1)
                m.matmul(ps_sum[:, b, :], ident[:, :], res_sb[:, b, :], start=True, stop=False)
                for n, (lo, hi) in enumerate(ph.dve_parts()):
                    pe.wait_ge(S["weighted"], j * ph.parts + (ph.parts_before + n + 1))
                    for k in range(lo, hi):
                        last = m.matmul(ps_sum[:, b, :], ident[:, :], gath[:, ph.slot(b, k), 0:HD],
                                        start=False, stop=False)
                    if not ph.loop:
                        last.then_inc(S["part_sum"], 1)
                for n in range(ph.act_slots):
                    k = K - ph.act_slots + n
                    pe.wait_ge(S["act_weighted"], j * ph.act_slots + (ph.act_before + n + 1))
                    last = m.matmul(ps_sum[:, b, :], ident[:, :], gath[:, ph.slot(b, k), 0:HD],
                                    start=False, stop=(k == K - 1))
                last.then_inc(S["tile_sum"], 1)

            for ph in phases:
                if not ph.loop:
                    tile_sums(ph, 0, ph.c0 % 2)
                else:
                    with pe.Fori(0, ph.n // 2) as i:
                        for q in range(2):
                            tile_sums(ph, 2 * i + q, (ph.c0 + q) % 2)

            pe.wait_ge(S["flag_b"], TILES - FIRST)
            m.transpose(ps_flag[0:TILES, 0:P], flags[:, :], ident[:, :]).then_inc(S["fl_t"], 1)
            pe.wait_ge(S["fl_max"], 1)
            m.matmul(ps_flag_row[0:1, 0:TILES], flagT[:, :], ident[0:TILES, 0:TILES], start=True, stop=True
                     ).then_inc(S["fl_row"], 1)

            pe.sem_inc(S["d_pv"], 2)
            pe.sem_inc(S["d_used"], 4)
            done = pe.alloc_register("dense_pe")
            pe.reg_mov(done, 0)
            pe.wait_ge(S["gr_ready"], 1)

            def dense_tile(pe, t):
                    n = pe.snap(done)

                    def turn_back(g, b):
                        hold(pe, S["d_ot"], g + 1)
                        m.transpose(ps_out[:, b, :], ot_sb[:, b, :], ident[0:D, 0:D]).then_inc(S["d_oT"], 1)

                    def head(h, b, landed, first=False):
                        g = n * H + h
                        pe.wait_ge(S[f"d_h{b}"], n * (16 * H // 2) + landed)
                        hv = h_sb[b][:, :].rearrange("p (c d) -> p c d", d=D)

                        def weighted(q):
                            pe.wait_ge(S["d_ev"], g * 16 + (q + 1))
                            for r in range(4):
                                last = m.matmul(ps_acc[:, b, :], hv[:, 4 * q + r, :],
                                                pt_sb[q % 4][:, r * P:(r + 1) * P], start=(q == 0 and r == 0),
                                                stop=(q == 15 and r == 3))
                            return last.then_inc(S["d_used"], 1)

                        for q in range(16):
                            if q % 8 == 0:
                                pe.wait_ge(S["d_exp"], g * 2 + (q // 8 + 1))
                            for r in range(4):
                                last = m.transpose(ps_pt[q % 4][:, r * P:(r + 1) * P],
                                                   u_sb[b][:, (4 * q + r) * P:(4 * q + r + 1) * P], ident[:, :])
                            last.then_inc(S["d_tr"], 1)
                            if q == 1 and not first:
                                turn_back(g - 1, 1 - b)
                            if q >= 2:
                                weighted(q - 2)
                        weighted(14)
                        weighted(15)
                        pe.wait_ge(S["d_used"], (g + 1) * 16 + 4)
                        pe.sem_inc(S["d_pv"], 1)
                        pe.sem_inc(S["d_acc"], 1)

                    head(0, 0, 16, first=True)
                    with pe.Fori(0, H // 2 - 1) as hp:
                        head(hp * 2 + 1, 1, hp * 16 + 16)
                        head(hp * 2 + 2, 0, hp * 16 + 32)
                    head(H - 1, 1, 16 * H // 2)
                    turn_back(n * H + (H - 1), 1)
                    pe.reg_add(done, done, 1)

            flagged_tiles(pe, dense_tile)


_INS = ["x", "adj", "L0_gnn_W", "L0_gnn_We", "L0_gnn_be", "L0_gnn_a_src", "L0_gnn_a_dst", "L0_gnn_Wr", "L0_gnn_br"]
_OUTS = [((N, HD), "float32")]


def kernel(**inputs):
    import numpy as _np
    import concourse.bacc as _bacc
    from concourse import mybir as _mybir
    from concourse.bass_utils import run_bass_kernel_spmd as _run

    nc = _bacc.Bacc("TRN2", target_bir_lowering=False, num_devices=1)
    arrays, args = {}, []
    for name in _INS:
        a = _np.ascontiguousarray(inputs[name])
        arrays[f"in_{name}_dram"] = a
        args.append(nc.dram_tensor(f"in_{name}_dram", a.shape, _mybir.dt.from_np(a.dtype), kind="ExternalInput").ap())
    for i, (shape, dtype) in enumerate(_OUTS):
        dt = _mybir.dt.from_np(_np.dtype(dtype))
        args.append(nc.dram_tensor(f"out_{i}_dram", shape, dt, kind="ExternalOutput").ap())
    gat_kernel(nc, *args)
    r = _run(nc, [arrays], core_ids=[0])
    got = tuple(r.results[0][f"out_{i}_dram"] for i in range(len(_OUTS)))
    return got[0]
```
